# Optimizing a Trainium2 kernel written in Bass

```python
import numpy as np
import jax
import jax.numpy as jnp

def _softmax(x, axis=-1):
    return jax.nn.softmax(x, axis=axis)

def _gelu(x):
    return jax.nn.gelu(x, approximate=True)

def _silu(x):
    return jax.nn.silu(x)

def _sigmoid(x):
    return jax.nn.sigmoid(x)

def _layernorm(x, axis=-1, eps=1e-05):
    m = jnp.mean(x, axis=axis, keepdims=True)
    v = jnp.var(x, axis=axis, keepdims=True)
    return (x - m) / jnp.sqrt(v + eps)

def _scatter_add(tgt, idx, src, axis=0):
    return tgt.at[idx].add(src)

def _segment_sum(src, seg, n):
    return jax.ops.segment_sum(src, seg, n)
kernel_name = 'mk_gnn_preln_d2_gnn_r8_7c23f2'

def setup_inputs(seed: int=0):
    np.random.seed(seed)
    _w = jnp.asarray

    def _rec_inputs():
        import jax
        import jax.numpy as jnp
        _gk = jax.random.key(seed)
        x = -0.0002117 + 1 * jax.random.normal(jax.random.fold_in(_gk, 1), (1250, 512), jnp.float32)
        src = jax.random.randint(jax.random.fold_in(_gk, 2), (20000,), 0, 1250, jnp.int32)
        dst = jnp.minimum((1250 * jax.random.uniform(jax.random.fold_in(_gk, 3), (20000,)) ** 2.0).astype(jnp.int32), 9999)
        _o = jnp.argsort(dst, stable=True)
        src = src[_o]
        dst = dst[_o]
        edge_attr_64 = 0.000279952 + 1.00013 * jax.random.normal(jax.random.fold_in(_gk, 11), (20000, 64), jnp.float32)
        return (x, src, dst, edge_attr_64)
    x, src, dst, edge_attr_64 = _rec_inputs()

    def _L0_gnn_setup():
        import jax, jax.numpy as jnp
        import numpy as np
        BN_EPS = 1e-05

        def batch_norm(h, gamma, beta):
            mu = jnp.mean(h, axis=0)
            var = jnp.var(h, axis=0)
            return (h - mu) * jax.lax.rsqrt(var + BN_EPS) * gamma + beta
        key = jax.random.key(seed)
        ks = jax.random.split(key, 6)
        N, E, dim = (6250, 200000, 512)
        hidden = dim * 2
        x = jax.random.normal(ks[0], (N, dim), dtype=jnp.float32)
        edge_index = jax.random.randint(ks[1], (2, E), 0, N, dtype=jnp.int64)
        s1 = 1.0 / np.sqrt(dim)
        s2 = 1.0 / np.sqrt(hidden)
        return {'x': x, 'edge_index': edge_index, 'eps': jnp.float32(0.0), 'W1': jax.random.uniform(ks[2], (dim, hidden), jnp.float32, -s1, s1), 'b1': jnp.zeros((hidden,), jnp.float32), 'g1': jnp.ones((hidden,), jnp.float32), 'be1': jnp.zeros((hidden,), jnp.float32), 'W2': jax.random.uniform(ks[3], (hidden, dim), jnp.float32, -s2, s2), 'b2': jnp.zeros((dim,), jnp.float32), 'g2': jnp.ones((dim,), jnp.float32), 'be2': jnp.zeros((dim,), jnp.float32)}
    _L0_gnn_all = _L0_gnn_setup()
    _L0_gnn_in = {k: v for k, v in _L0_gnn_all.items() if k in ('eps', 'W1', 'b1', 'g1', 'be1', 'W2', 'b2', 'g2', 'be2')}
    del _L0_gnn_all

    def _L1_gnn_setup():
        import jax, jax.numpy as jnp
        import numpy as np
        N_NODES = 2500
        N_EDGES = 40000
        HIDDEN = 512
        EDGE_DIM = 64
        LN_EPS = 1e-05

        def mish(x):
            return x * jnp.tanh(jax.nn.softplus(x))
        key = jax.random.key(seed)
        ks = jax.random.split(key, 8)
        s = lambda fan_in: 1.0 / np.sqrt(fan_in)
        return {'x': jax.random.normal(ks[0], (N_NODES, HIDDEN), dtype=jnp.float32), 'edge_index': jax.random.randint(ks[1], (2, N_EDGES), 0, N_NODES, dtype=jnp.int64), 'edge_attr': jax.random.normal(ks[2], (N_EDGES, EDGE_DIM), dtype=jnp.float32), 'W1': jax.random.normal(ks[3], (2 * HIDDEN + EDGE_DIM, HIDDEN), dtype=jnp.float32) * s(2 * HIDDEN + EDGE_DIM), 'b1': jnp.zeros((HIDDEN,), dtype=jnp.float32), 'W2': jax.random.normal(ks[4], (HIDDEN, HIDDEN), dtype=jnp.float32) * s(HIDDEN), 'b2': jnp.zeros((HIDDEN,), dtype=jnp.float32), 'W3': jax.random.normal(ks[5], (2 * HIDDEN, HIDDEN), dtype=jnp.float32) * s(2 * HIDDEN), 'b3': jnp.zeros((HIDDEN,), dtype=jnp.float32), 'W4': jax.random.normal(ks[6], (HIDDEN, HIDDEN), dtype=jnp.float32) * s(HIDDEN), 'b4': jnp.zeros((HIDDEN,), dtype=jnp.float32), 'gamma': jnp.ones((HIDDEN,), dtype=jnp.float32), 'beta': jnp.zeros((HIDDEN,), dtype=jnp.float32)}
    _L1_gnn_all = _L1_gnn_setup()
    _L1_gnn_in = {k: v for k, v in _L1_gnn_all.items() if k in ('W1', 'b1', 'W2', 'b2', 'W3', 'b3', 'W4', 'b4', 'gamma', 'beta')}
    del _L1_gnn_all
    return {'x': x, 'src': src, 'dst': dst, 'edge_attr_64': edge_attr_64, 'L0_gnn_eps': _L0_gnn_in['eps'], 'L0_gnn_W1': _L0_gnn_in['W1'], 'L0_gnn_b1': _L0_gnn_in['b1'], 'L0_gnn_g1': _L0_gnn_in['g1'], 'L0_gnn_be1': _L0_gnn_in['be1'], 'L0_gnn_W2': _L0_gnn_in['W2'], 'L0_gnn_b2': _L0_gnn_in['b2'], 'L0_gnn_g2': _L0_gnn_in['g2'], 'L0_gnn_be2': _L0_gnn_in['be2'], 'L1_gnn_W1': _L1_gnn_in['W1'], 'L1_gnn_b1': _L1_gnn_in['b1'], 'L1_gnn_W2': _L1_gnn_in['W2'], 'L1_gnn_b2': _L1_gnn_in['b2'], 'L1_gnn_W3': _L1_gnn_in['W3'], 'L1_gnn_b3': _L1_gnn_in['b3'], 'L1_gnn_W4': _L1_gnn_in['W4'], 'L1_gnn_b4': _L1_gnn_in['b4'], 'L1_gnn_gamma': _L1_gnn_in['gamma'], 'L1_gnn_beta': _L1_gnn_in['beta']}

def reference(x, src, dst, edge_attr_64, L0_gnn_eps, L0_gnn_W1, L0_gnn_b1, L0_gnn_g1, L0_gnn_be1, L0_gnn_W2, L0_gnn_b2, L0_gnn_g2, L0_gnn_be2, L1_gnn_W1, L1_gnn_b1, L1_gnn_W2, L1_gnn_b2, L1_gnn_W3, L1_gnn_b3, L1_gnn_W4, L1_gnn_b4, L1_gnn_gamma, L1_gnn_beta):
    import jax
    import jax.numpy as jnp

    def _L0_gnn_ref(x, edge_index, eps, W1, b1, g1, be1, W2, b2, g2, be2):
        import jax, jax.numpy as jnp
        import numpy as np
        BN_EPS = 1e-05

        def batch_norm(h, gamma, beta):
            mu = jnp.mean(h, axis=0)
            var = jnp.var(h, axis=0)
            return (h - mu) * jax.lax.rsqrt(var + BN_EPS) * gamma + beta
        N = x.shape[0]
        src, dst = (edge_index[0], edge_index[1])
        agg = jax.ops.segment_sum(x[src], dst, num_segments=N)
        h = (1.0 + eps) * x + agg
        h = jax.nn.relu(batch_norm(h @ W1 + b1, g1, be1))
        h = h @ W2 + b2
        h = jax.nn.relu(batch_norm(h, g2, be2))
        return x + h

    def _L1_gnn_ref(x, edge_index, edge_attr, W1, b1, W2, b2, W3, b3, W4, b4, gamma, beta):
        import jax, jax.numpy as jnp
        import numpy as np
        N_NODES = 2500
        N_EDGES = 40000
        HIDDEN = 512
        EDGE_DIM = 64
        LN_EPS = 1e-05

        def mish(x):
            return x * jnp.tanh(jax.nn.softplus(x))
        src, dst = (edge_index[0], edge_index[1])
        edge_feat = jnp.concatenate([x[src], x[dst], edge_attr], axis=-1)
        h = mish(edge_feat @ W1 + b1)
        messages = mish(h @ W2 + b2)
        agg = jax.ops.segment_sum(messages, dst, num_segments=x.shape[0])
        u = mish(jnp.concatenate([x, agg], axis=-1) @ W3 + b3)
        out = u @ W4 + b4
        y = x + out
        mu = jnp.mean(y, axis=-1, keepdims=True)
        var = jnp.mean(jnp.square(y - mu), axis=-1, keepdims=True)
        return (y - mu) * jax.lax.rsqrt(var + LN_EPS) * gamma + beta
    edge_index = jnp.stack([src, dst])
    h = jnp.maximum(_layernorm(x, axis=-1), 0.0)
    x = x + _L0_gnn_ref(h, edge_index, L0_gnn_eps, L0_gnn_W1, L0_gnn_b1, L0_gnn_g1, L0_gnn_be1, L0_gnn_W2, L0_gnn_b2, L0_gnn_g2, L0_gnn_be2)
    h = jnp.maximum(_layernorm(x, axis=-1), 0.0)
    x = x + _L1_gnn_ref(h, edge_index, edge_attr_64, L1_gnn_W1, L1_gnn_b1, L1_gnn_W2, L1_gnn_b2, L1_gnn_W3, L1_gnn_b3, L1_gnn_W4, L1_gnn_b4, L1_gnn_gamma, L1_gnn_beta)
    return x

_drawn_inputs = setup_inputs


def setup_inputs(seed=0):
    import zlib

    import numpy as np

    out = dict(_drawn_inputs(seed))
    spreads = {'L0_gnn_b1': (0.0, 0.8),
     'L0_gnn_g1': (1.0, 0.2),
     'L0_gnn_be1': (0.0, 0.1),
     'L0_gnn_b2': (0.0, 0.8),
     'L0_gnn_g2': (1.0, 0.2),
     'L0_gnn_be2': (0.0, 0.1),
     'L1_gnn_b1': (0.0, 0.1),
     'L1_gnn_b2': (0.0, 0.1),
     'L1_gnn_b3': (0.0, 0.416),
     'L1_gnn_b4': (0.0, 0.291),
     'L1_gnn_gamma': (1.0, 0.2),
     'L1_gnn_beta': (0.0, 0.1)}
    factors = {}
    for name, (base, spread) in spreads.items():
        noise = np.random.default_rng([zlib.crc32(name.encode()), seed]).standard_normal(out[name].shape)
        drawn = base * np.exp(spread * noise) if base else spread * noise
        out[name] = jnp.asarray(drawn.astype(out[name].dtype))
    for name, factor in factors.items():
        out[name] = (out[name] * factor).astype(out[name].dtype)
    return out
```

```python
from contextlib import ExitStack

import concourse.bass as bass
from concourse import mybir

ALU = mybir.AluOpType
ACT = mybir.ActivationFunctionType
F32 = mybir.dt.float32
F32R = mybir.dt.float32r
I32 = mybir.dt.int32
AX = mybir.AxisListType

P = 128
NODES, DIM, HID0, EDGE_DIM = 1250, 512, 1024, 64
EDGES = 20000
NT = -(-NODES // P)
NP = NT * P
KD = DIM // P
KH = HID0 // P
GROUP = 4
RING = 4
TILES = -(-EDGES // (GROUP * RING * P)) * GROUP * RING
GROUPS = TILES // GROUP
PAIRS = TILES // 2
R_LOW, R_EXTRA, R_HIGH, R_WORDS = 0, 2, 4, 8
PW = 2 * P
BLOCKS = 4
BW = NP // BLOCKS
LN_EPS = BN_EPS = 1e-5
E_MAX = 1e9
Z_MAX = 20.0
BN_PIECES = [(0, 512), (512, 1024), (1024, NODES)]
CB1, CG1, CBE1, CB2, CG2, CBE2, CB3 = 0, 8, 16, 24, 28, 32, 36
NCOLS = 40
ROW_B1, ROW_B2, ROW_B4, ROW_GAMMA, ROW_BETA = range(5)


def gnn_kernel(nc, x, src_cols, dst_cols, dst_rows, edge_attr_t, eps, cols, rows, w01, w02,
               w1, w2, w3, w4, out):
    ctx = ExitStack()
    with ctx:
        place = [nc.sbuf_base + (-nc.sbuf_base) % 64]

        def sb(name, shape, dt=F32, at=None):
            size = 4
            for n in shape[1:]:
                size *= n
            if at is None:
                at = place[0]
                place[0] += size + (-size) % 32
            return nc.alloc_sbuf_tensor_at(name, shape, dt, offset=at), at + size + (-size) % 32

        X, _ = sb("x_nodes", [P, NT, DIM])
        H, _ = sb("h_nodes", [P, NT, DIM])
        AGG, _ = sb("agg_nodes", [P, NT, DIM])
        t1_at = place[0]
        T1, _ = sb("act_t", [P, KD, NP])
        h1t_at = place[0]
        H1T, _ = sb("hidden_t", [P, KH, NP])
        WA, _ = sb("weights_a", [P, 2 * KD, DIM])
        WB, _ = sb("weights_b", [P, 2 * KD, DIM])
        W4 = WA[:, 0:KD, :]
        XWORK = WA[:, KD, 0:BW]
        W2_HI, _ = sb("w2_hi", [P, KD, DIM], F32R)
        W2_LO, _ = sb("w2_lo", [P, KD, DIM], F32R)
        WE_HI, _ = sb("we_hi", [P, DIM], F32R)
        WE_LO, _ = sb("we_lo", [P, DIM], F32R)
        B2_R, _ = sb("b2_parts", [64, DIM], F32R)
        ONES_R, _ = sb("ones", [64, P], F32R)
        ROWS, _ = sb("rows", [P, 5, DIM])
        IOTA, _ = sb("iota", [P, NP])
        IDENT, _ = sb("ident", [P, P])
        SRC, _ = sb("src", [P, TILES], I32)
        DST, _ = sb("dst", [P, TILES], I32)
        DSTF, _ = sb("dst_f", [P, TILES])
        RANGE, _ = sb("tile_range", [1, R_WORDS * PAIRS], I32)
        IDX, _ = sb("gather_index", [P, RING, 4], I32)
        ONEHOT, _ = sb("onehot", [P, 2, P])
        XHOT, _ = sb("onehot_extra", [P, P])
        COLS, _ = sb("cols", [P, NCOLS])
        STATS, _ = sb("stats", [P, NT, 6])
        BSTATS, _ = sb("bn_stats", [P, KH, 18])
        MV, _ = sb("bn_mean_var", [P, KH, 2])
        MEAN, _ = sb("mean", [P, NT])
        VAR, _ = sb("var", [P, NT])
        RSTD, _ = sb("rstd", [P, NT])
        TMP, _ = sb("tmp", [P, 5, NT])
        SCALE, _ = sb("bn_scale", [P, KH])
        SHIFT, _ = sb("bn_shift", [P, KH])
        EPS1, _ = sb("eps1", [P, 1])
        CONST, _ = sb("consts", [P, 2])
        assert place[0] <= nc.sbuf_usable_end, place[0] - nc.sbuf_usable_end
        ROWS0, at = sb("gather_h", [P, RING, GROUP, DIM], at=t1_at)
        HOT0, at = sb("onehot_0", [P, 2, GROUP, P], at=at)
        W2_RAW, at = sb("w2_raw", [P, KD, DIM], at=at)
        WE_RAW, at = sb("we_raw", [P, DIM], at=at)
        DROW, at = sb("dst_tiles", [PAIRS, 2, P], I32, at=at)
        RNG_T, at = sb("range_tiles", [PAIRS, R_WORDS], I32, at=at)
        assert at <= h1t_at + 4 * KH * NP
        QST, _ = sb("q_stage", [P, NT, DIM], at=h1t_at)
        GQ, at = sb("gather_q", [P, 4, DIM], at=t1_at)
        EA, at = sb("mish1_work", [P, KD, PW], at=at)
        EB, at = sb("mish2_work", [P, 2, DIM], at=at)
        HF, at = sb("h_full", [P, KD, PW], at=at)
        GP, at = sb("gather_p", [P, 4, DIM], at=at)
        H_HI, at = sb("h_hi", [P, 2, KD, PW], F32R, at=at)
        H_LO, at = sb("h_lo", [P, 2, KD, PW], F32R, at=at)
        MSG, at = sb("message", [P, 2, DIM], at=at)
        AT_RAW, at = sb("edge_attr", [P, 2, PW], at=at)
        AT_R, at = sb("edge_attr_parts", [P, 2, PW], F32R, at=at)
        assert at <= h1t_at + 4 * KH * NP
        AT2, _ = sb("agg_t", [P, KD, NP], at=h1t_at)
        UT, _ = sb("u_t", [P, KD, NP], at=h1t_at + 4 * KD * NP)

        BANKS = ctx.enter_context(nc.psum_tensor("banks", [P, 8, 512], F32))
        Z1, SEG, Z2 = BANKS[:, 0:2, :], BANKS[:, 2:4, :], BANKS[:, 4:8, :]
        Z1v = Z1[:, :, :].rearrange("p b (c e) -> p (b c) e", c=2)

        h_tab = nc.dram_tensor("h_table", [NP, DIM], F32)
        p_tab = nc.dram_tensor("p_table", [NP, DIM], F32)
        q_tab = nc.dram_tensor("q_table", [NP, DIM], F32)
        r_tab = nc.dram_tensor("range_table", [PAIRS, R_WORDS], I32)

        def sem(name):
            return ctx.enter_context(nc.semaphore(name))

        x_in, idx_in, small_in, w01_in, w02_in = (sem(n) for n in
            ("x_in", "idx_in", "small_in", "w01_in", "w02_in"))
        split_in, w1_in, w3_in, w4_in = (sem(n) for n in ("split_in", "w1_in", "w3_in", "w4_in"))
        range_out, range_in, range_ready = (sem(n) for n in ("range_out", "range_in", "range_ready"))
        pool_const, dve_const, dve_chain = (sem(n) for n in ("pool_const", "dve_const", "dve_chain"))
        var_ready, std_ready, h_ready, h_stored = (sem(n) for n in
            ("var_ready", "std_ready", "h_ready", "h_stored"))
        norm_done = sem("norm_done")
        idx_copied = sem("idx_copied")
        gat0 = [sem(f"gathered0_{g}") for g in range(RING)]
        gat1 = [sem(f"gathered1_{j}") for j in range(2)]
        hot_ready, seg_done, agg_done = sem("hot_ready"), sem("seg_done"), sem("agg_done")
        xhot_ready, xseg_done, xagg_done = sem("xhot_ready"), sem("xseg_done"), sem("xagg_done")
        z0_ready = sem("z0_ready")
        tr_done, tr_moved = sem("tr_done"), sem("tr_moved")
        mm_done, mm_moved = sem("mm_done"), sem("mm_moved")
        bn_ready, bn_applied = sem("bn_ready"), sem("bn_applied")
        q_moved, pq_stored = sem("q_moved"), sem("pq_stored")
        attr_in = [sem(f"attr_in{j}") for j in range(2)]
        attr_hi, attr_ready = sem("attr_hi"), sem("attr_ready")
        z1_done, a_exp, a_cut, a_sq, a_ln, a_r, h_full, h_hi, h_lo = ([sem(f"{n}_{h}") for h in range(2)] for n in
            ("z1_done", "a_exp", "a_cut", "a_sq", "a_ln", "a_r", "h_full", "h_hi", "h_lo"))
        z2_done = sem("z2_done")
        b_exp, b_cut, b_sq, b_ln, b_r, msg_ready = (sem(n) for n in
            ("b_exp", "b_cut", "b_sq", "b_ln", "b_r", "msg_ready"))
        u_bias, u_exp, u_cut, u_sq, u_ln, u_r, u_ready = (sem(n) for n in
            ("u_bias", "u_exp", "u_cut", "u_sq", "u_ln", "u_r", "u_ready"))
        y_done, y_moved, out_ready, out_stored = (sem(n) for n in
            ("y_done", "y_moved", "out_ready", "out_stored"))

        block = ctx.enter_context(nc.Block())

        def pair_range(s, word, n):
            return RANGE[0:1, bass.ds(R_WORDS * s + word, n)]

        TR_Z0, TR_R2, TR_H2, TR_AGG = (NT * n for n in range(4))
        TR_H3 = 4 * NT
        SUMS0, SUMS1 = 1, TILES + 2
        MM_1 = 0
        FREE = 4
        MM_2 = BLOCKS * KH
        MM_PQ = MM_2 + BLOCKS * KD

        @block.sync
        def _(sp):
            sp.dma_start(X[:, :, :], x.rearrange("(t p) d -> p t d", p=P)).then_inc(x_in, 16)
            sp.dma_start(DROW[:, :, :], dst_rows).then_inc(idx_in, 16)
            sp.dma_start(SRC[:, :], src_cols).then_inc(idx_in, 16)
            sp.dma_start(DST[:, :], dst_cols).then_inc(idx_in, 16)
            sp.dma_start(COLS[:, :], cols).then_inc(small_in, 16)
            sp.dma_start(EPS1[:, :], eps.partition_broadcast(P)).then_inc(small_in, 16)
            sp.dma_start(ROWS[:, :, :], rows.partition_broadcast(P)).then_inc(small_in, 16)
            sp.wait_ge(range_ready, 1)
            sp.dma_start(r_tab[:, :], RNG_T[:, :]).then_inc(range_out, 16)
            sp.wait_ge(range_out, 16)
            sp.dma_start(RANGE[0:1, :], r_tab.rearrange("(o s) j -> o (s j)", o=1)).then_inc(range_in, 16)
            sp.dma_start(W2_RAW[:, :, :], w2.rearrange("(k p) n -> p k n", p=P)).then_inc(split_in, 16)
            for half in range(2):
                sp.dma_start(WE_RAW[EDGE_DIM * half:EDGE_DIM * (half + 1), :], w1[2 * DIM:, :]).then_inc(split_in, 16)
            sp.wait_ge(h_ready, 1)
            sp.dma_start(h_tab.rearrange("(t p) d -> p t d", p=P), H[:, :, :]).then_inc(h_stored, 16)
            sp.dma_start(WA[:, :, :].rearrange("p a n -> p (a n)").rearrange("p (k n) -> p k n", k=KD),
                         w01.rearrange("(k p) n -> p k n", p=P)).then_inc(w01_in, 16)
            sp.dma_start(WB[:, :, :], w02.rearrange("(k p) n -> p k n", p=P)).then_inc(w02_in, 16)
            sp.wait_ge(mm_done, MM_2)
            sp.dma_start(WA[:, :, :], w1[0:2 * DIM, :].rearrange("(k p) n -> p k n", p=P)).then_inc(w1_in, 16)
            sp.wait_ge(mm_done, MM_PQ)
            sp.dma_start(WB[:, :, :], w3.rearrange("(k p) n -> p k n", p=P)).then_inc(w3_in, 16)
            sp.wait_ge(mm_moved, FREE + MM_PQ + NT)
            sp.dma_start(p_tab.rearrange("(t p) d -> p t d", p=P), AGG[:, :, :]).then_inc(pq_stored, 16)
            sp.wait_ge(q_moved, NT)
            sp.dma_start(q_tab.rearrange("(t p) d -> p t d", p=P), QST[:, :, :]).then_inc(pq_stored, 16)
            sp.dma_start(W4, w4.rearrange("(k p) n -> p k n", p=P)).then_inc(w4_in, 16)
            sp.wait_ge(pq_stored, 32)
            for j in range(2):
                sp.dma_start(AT_RAW[:, j, :], edge_attr_t[j, :, :]).then_inc(attr_in[j], 16)
            with sp.Fori(1, PAIRS // 2) as i:
                for j in range(2):
                    sp.wait_ge(attr_ready, 2 * i + j - 1)
                    sp.dma_start(AT_RAW[:, j, :], edge_attr_t[bass.ds(2 * i + j, 1), :, :]
                                 .rearrange("o p e -> (o p) e")).then_inc(attr_in[j], 16)
            for nt in range(NT):
                n = min(P, NODES - nt * P)
                sp.wait_ge(out_ready, nt + 1)
                sp.dma_start(out[nt * P:nt * P + n, :], H[0:n, nt, :]).then_inc(out_stored, 16)
            sp.wait_ge(out_stored, 16 * NT)

        @block.gpsimd
        def _(pool):
            nc.gpsimd.memset(IDENT[:, :], 0.0).then_inc(pool_const, 1)
            nc.gpsimd.iota(IOTA[:, :], [[1, NP]], base=0, channel_multiplier=0,
                           allow_small_or_imprecise_dtypes=True).then_inc(pool_const, 1)
            pool.wait_ge(pool_const, 2)
            nc.gpsimd.affine_select(out=IDENT[:, :], in_=IDENT[:, :], compare_op=ALU.not_equal, fill=1.0,
                                    base=0, pattern=[[-1, P]], channel_multiplier=1).then_inc(pool_const, 1)
            pool.wait_ge(idx_in, 48)
            held = [pool.alloc_register(f"pool_held{n}") for n in range(2)]

            def reached(n, value):
                if isinstance(value, int):
                    return value
                pool.reg_mov(held[n], value)
                return pool.snap(held[n])

            pool.wait_ge(h_stored, 16)

            def gather0(i, first):
                for g in range(RING):
                    n = RING * i + g
                    summed, copied = reached(0, SUMS0 + GROUP * (n - RING + 1)), reached(1, n + 1)
                    pool.wait_ge(idx_in, 48)
                    if not first:
                        pool.wait_ge(agg_done, summed)
                    nc.gpsimd.tensor_copy(IDX[:, g, :], SRC[:, bass.ds(GROUP * n, GROUP)]).then_inc(idx_copied, 1)
                    pool.wait_ge(h_stored, 16)
                    pool.wait_ge(idx_copied, copied)
                    for j in range(GROUP):
                        nc.gpsimd.indirect_dma_start(
                            ROWS0[:, g, j, :], None, h_tab[:, :],
                            bass.IndirectOffsetOnAxis(ap=IDX[:, g, j:j + 1], axis=0)).then_inc(gat0[g], 16)

            gather0(0, True)
            with pool.Fori(1, GROUPS // RING) as i:
                gather0(i, False)

            pool.wait_ge(pq_stored, 32)
            pool.wait_ge(agg_done, SUMS0 + TILES)

            def gather1(i, j, first):
                s = 2 * i + j
                in_psum, copied = reached(0, s - 1), reached(1, GROUPS + 2 * (s + 1))
                pool.wait_ge(idx_in, 48)
                if not first:
                    pool.wait_ge(z1_done[1], in_psum)
                nc.gpsimd.tensor_copy(IDX[:, j, 0:2], SRC[:, bass.ds(2 * s, 2)]).then_inc(idx_copied, 1)
                nc.gpsimd.tensor_copy(IDX[:, j, 2:4], DST[:, bass.ds(2 * s, 2)]).then_inc(idx_copied, 1)
                pool.wait_ge(pq_stored, 32)
                pool.wait_ge(idx_copied, copied)
                for k in range(2):
                    for tab, rows_at, c in ((p_tab, GP, k), (q_tab, GQ, 2 + k)):
                        nc.gpsimd.indirect_dma_start(
                            rows_at[:, 2 * j + k, :], None, tab[:, :],
                            bass.IndirectOffsetOnAxis(ap=IDX[:, j, c:c + 1], axis=0)).then_inc(gat1[j], 16)

            for j in range(2):
                gather1(0, j, True)
            with pool.Fori(1, PAIRS // 2) as i:
                for j in range(2):
                    gather1(i, j, False)

        @block.tensor
        def _(pe):
            extras = pe.alloc_register("pe_extras")
            pe.reg_mov(extras, 1)
            more = [pe.alloc_register(f"pe_more{n}") for n in range(2)]

            def load_extra(n, s):
                pe.load(more[n], pair_range(s, R_EXTRA, 1))
                return pe.snap(more[n])

            def extra_tiles(s, j, bank, rows, added):
                low = pe.value_load(pair_range(s, R_LOW + j, 1), min_val=0, max_val=NT - 1)
                high = pe.value_load(pair_range(s, R_HIGH + j, 1), min_val=0, max_val=NT - 1)
                with pe.If(low < high):
                    with pe.Fori(low + 1, high + 1) as _:
                        n = pe.snap(extras)
                        pe.wait_ge(agg_done, added)
                        pe.wait_ge(xagg_done, n)
                        pe.wait_ge(xhot_ready, n + 1)
                        pe.matmul(bank, XHOT[:, :], rows, start=True, stop=True).then_inc(xseg_done, 1)
                        pe.reg_add(extras, extras, 1)

            pe.wait_ge(range_in, 16)

            with pe.Fori(0, GROUPS // RING) as i:
                for g in range(RING):
                    n = RING * i + g
                    more_tiles = load_extra(0, 2 * n) + load_extra(1, 2 * n + 1)
                    pe.wait_ge(gat0[g], 16 * GROUP * (i + 1))
                    pe.wait_ge(hot_ready, GROUP * (n + 1))
                    for j in range(GROUP):
                        pe.matmul(BANKS[:, GROUP * (g % 2) + j, :], HOT0[:, g % 2, j, :], ROWS0[:, g, j, :],
                                  start=True, stop=True).then_inc(seg_done, 1)
                    with pe.If(more_tiles > 0):
                        for j in range(GROUP):
                            extra_tiles(2 * n + j // 2, j % 2, BANKS[:, GROUP * (g % 2), :], ROWS0[:, g, j, :],
                                        SUMS0 + GROUP * n + 1)

            moves = [0]

            def transposes(source, ready, count, back=False):
                pe.wait_ge(ready, count)
                for nt in range(NT):
                    n = moves[0]
                    if n >= 2:
                        pe.wait_ge(tr_moved, n - 1)
                    for c in range(KD):
                        view = source[:, c, nt * P:(nt + 1) * P] if back else source[:, nt, c * P:(c + 1) * P]
                        mm = pe.transpose(SEG[:, n % 2, c * P:(c + 1) * P], view, IDENT[:, :])
                    mm.then_inc(tr_done, 1)
                    moves[0] += 1

            def product_t(base, weights, acts, kn, on):
                with pe.Fori(0, BLOCKS) as b:
                    for o in range(on):
                        pe.wait_ge(mm_moved, base + on * b + o + 1)
                        for k in range(kn):
                            mm = pe.matmul(Z2[:, o % 4, 0:BW], weights(k, o), acts(k, b), start=(k == 0), stop=(k == kn - 1))
                        mm.then_inc(mm_done, 1)

            WA0 = WA[:, :, :].rearrange("p a n -> p (a n)").rearrange("p (k n) -> p k n", k=KD)
            pe.wait_ge(pool_const, 3)
            transposes(AGG, z0_ready, 1)
            pe.wait_ge(w01_in, 16)
            pe.wait_ge(tr_moved, moves[0])
            product_t(MM_1, lambda k, o: WA0[:, k, o * P:(o + 1) * P],
                      lambda k, b: T1[:, k, bass.ds(b * BW, BW)], KD, KH)
            pe.wait_ge(w02_in, 16)
            pe.wait_ge(bn_applied, KH)
            product_t(MM_2, lambda k, o: WB[:, k, o * P:(o + 1) * P],
                      lambda k, b: H1T[:, k, bass.ds(b * BW, BW)], KH, KD)
            transposes(T1, bn_applied, KH + KD, back=True)
            transposes(H, h_ready, 2)

            pe.wait_ge(w1_in, 16)
            pe.wait_ge(tr_moved, moves[0])
            for nt in range(NT):
                for part, moved, base in ((0, mm_moved, FREE + MM_PQ), (1, q_moved, 0)):
                    if nt >= 2:
                        pe.wait_ge(moved, base + nt - 1)
                    for k in range(KD):
                        mm = pe.matmul(Z2[:, 2 * part + nt % 2, :], T1[:, k, nt * P:(nt + 1) * P],
                                       WA[:, KD * part + k, :], start=(k == 0), stop=(k == KD - 1))
                    mm.then_inc(mm_done, 1)
            pe.wait_ge(mm_moved, FREE + MM_PQ + NT)
            pe.wait_ge(q_moved, NT)

            def z1(s, i, j):
                pe.wait_ge(gat1[j], 64 * (i + 1))
                for b in range(2):
                    if not (isinstance(s, int) and s == 0):
                        pe.wait_ge(h_full[b], s)
                    for rows_at in (GP, GQ):
                        for c in (2 * b, 2 * b + 1):
                            for k in range(2):
                                pe.matmul(Z1v[:, c, k * P:(k + 1) * P], rows_at[:, 2 * j + k, c * P:(c + 1) * P],
                                          IDENT[:, :], is_transpose=True, skip_group_check=True,
                                          start=(rows_at is GP and c == 2 * b and k == 0), stop=False)
                    pe.wait_ge(attr_ready, s + 1)
                    for c in (2 * b, 2 * b + 1):
                        for w in (WE_HI, WE_LO):
                            mm = pe.matmul(Z1v[:, c, :], w[:, c * P:(c + 1) * P], AT_R[:, j, :],
                                           skip_group_check=True, start=False, stop=(w is WE_LO and c == 2 * b + 1))
                    mm.then_inc(z1_done[b], 1)

            def z2(s, j):
                if not isinstance(s, int) or s >= 2:
                    pe.wait_ge(msg_ready, 1 + s - 1)
                pe.wait_ge(h_lo[0], s + 1)
                pe.wait_ge(h_lo[1], s + 1)
                for k in range(2):
                    at = Z2[:, 2 * j + k, :]
                    pe.matmul(at, ONES_R[:, :], B2_R[:, :], start=True, stop=False)
                    for c in range(KD):
                        e = slice(k * P, (k + 1) * P)
                        pe.matmul(at, H_LO[:, j, c, e], W2_HI[:, c, :], start=False, stop=False)
                        pe.matmul(at, H_HI[:, j, c, e], W2_LO[:, c, :], start=False, stop=False)
                        mm = pe.matmul(at, H_HI[:, j, c, e], W2_HI[:, c, :], start=False, stop=(c == KD - 1))
                mm.then_inc(z2_done, 1)

            def segment1(s, more_tiles):
                pe.wait_ge(msg_ready, 1 + s + 1)
                for j in range(2):
                    pe.matmul(SEG[:, j, :], ONEHOT[:, j, :], MSG[:, j, :], start=True, stop=True).then_inc(seg_done, 1)
                with pe.If(more_tiles > 0):
                    for j in range(2):
                        extra_tiles(s, j, SEG[:, 0, :], MSG[:, j, :], SUMS1 + 2 * s + 1)

            z1(0, 0, 0)
            z1(1, 0, 1)
            z2(0, 0)
            with pe.Fori(1, PAIRS // 2) as i:
                for j in range(2):
                    s = 2 * i + j
                    more_tiles = load_extra(0, s - 2)
                    z1(s, i, j)
                    z2(s - 1, 1 - j)
                    segment1(s - 2, more_tiles)
            z2(PAIRS - 1, 1)
            segment1(PAIRS - 2, load_extra(0, PAIRS - 2))
            segment1(PAIRS - 1, load_extra(0, PAIRS - 1))

            transposes(AGG, agg_done, SUMS1 + TILES)
            transposes(H, h_ready, 2)
            pe.wait_ge(w3_in, 16)
            pe.wait_ge(tr_moved, moves[0])
            with pe.Fori(0, BLOCKS) as b:
                for o in range(KD):
                    pe.wait_ge(u_ready, KD * (b + 1))
                    for k in range(2 * KD):
                        a = (T1 if k < KD else AT2)[:, k % KD, bass.ds(b * BW, BW)]
                        mm = pe.matmul(Z2[:, o, 0:BW], WB[:, k, o * P:(o + 1) * P], a, start=(k == 0), stop=(k == 2 * KD - 1))
                    mm.then_inc(mm_done, 1)
            pe.wait_ge(u_ready, KD * (BLOCKS + 1))
            pe.wait_ge(w4_in, 16)
            for nt in range(NT):
                if nt >= 2:
                    pe.wait_ge(y_moved, nt - 1)
                for k in range(KD):
                    mm = pe.matmul(Z2[:, nt % 2, :], UT[:, k, nt * P:(nt + 1) * P], W4[:, k, :],
                                   start=(k == 0), stop=(k == KD - 1))
                mm.then_inc(y_done, 1)

        @block.scalar
        def _(act):
            def std(n, var, count):
                act.wait_ge(var_ready, count)
                nc.scalar.activation(TMP[:, 3, 0:n], var, ACT.Sqrt, bias=CONST[:, 1:2]).then_inc(std_ready, 1)

            moves = [0]

            def move_t(target, scale=1.0):
                for nt in range(NT):
                    n = moves[0]
                    act.wait_ge(tr_done, n + 1)
                    nc.scalar.mul(target[:, :, nt * P:(nt + 1) * P],
                                  SEG[:, n % 2, :].rearrange("p (c e) -> p c e", c=KD), scale).then_inc(tr_moved, 1)
                    moves[0] += 1

            def move_product(base, target, on, bias):
                with act.Fori(0, BLOCKS) as b:
                    for o in range(on):
                        act.wait_ge(mm_done, base + on * b + o + 1)
                        nc.scalar.activation(target[:, o, bass.ds(b * BW, BW)], Z2[:, o % 4, 0:BW], ACT.Identity,
                                             bias=COLS[:, bias + o:bias + o + 1]).then_inc(mm_moved, 1)

            def apply_bn(target, on, count):
                act.wait_ge(bn_ready, count)
                for o in range(on):
                    nc.scalar.activation(target[:, o, :], target[:, o, :], ACT.Relu, bias=SHIFT[:, o:o + 1],
                                         scale=SCALE[:, o:o + 1]).then_inc(bn_applied, 1)

            act.wait_ge(dve_const, 1)
            act.wait_ge(small_in, 48)
            std(NT, VAR[:, :], 1)
            move_t(T1)
            move_product(MM_1, H1T, KH, CB1)
            std(KH, MV[:, 0:KH, 1], 2)
            apply_bn(H1T, KH, 1)
            move_product(MM_2, T1, KD, CB2)
            std(KD, MV[:, 0:KD, 1], 3)
            apply_bn(T1, KD, 2)
            moves[0] += NT
            std(NT, VAR[:, :], 4)
            move_t(T1)
            for nt in range(NT):
                act.wait_ge(mm_done, MM_PQ + 2 * nt + 1)
                nc.scalar.copy(AGG[:, nt, :], Z2[:, nt % 2, :]).then_inc(mm_moved, 1)

            nc.scalar.preload_act_table_set("natural_log_exp_and_others")

            def exp1(s, h):
                act.wait_ge(z1_done[h], s + 1)
                if not (isinstance(s, int) and s == 0):
                    act.wait_ge(h_full[h], s)
                nc.scalar.activation(EA[:, 2 * h:2 * h + 2, :], Z1v[:, 2 * h:2 * h + 2, :], ACT.Exp).then_inc(a_exp[h], 1)

            def log1(s, h):
                act.wait_ge(a_sq[h], s + 1)
                nc.scalar.activation(EA[:, 2 * h:2 * h + 2, :], EA[:, 2 * h:2 * h + 2, :], ACT.Ln, bias=CONST[:, 0:1]).then_inc(a_ln[h], 1)

            def inv1(s, h):
                act.wait_ge(a_ln[h], s + 1)
                nc.scalar.activation(EA[:, 2 * h:2 * h + 2, :], EA[:, 2 * h:2 * h + 2, :], ACT.Exp, scale=-1.0).then_inc(a_r[h], 1)

            def hi1(s, j, h):
                act.wait_ge(h_full[h], s + 1)
                if not isinstance(s, int) or s >= 2:
                    act.wait_ge(z2_done, s - 1)
                nc.scalar.copy(H_HI[:, j, 2 * h:2 * h + 2, :], HF[:, 2 * h:2 * h + 2, :]).then_inc(h_hi[h], 1)

            def exp2(s, j):
                act.wait_ge(z2_done, s + 1)
                act.wait_ge(msg_ready, 1 + s)
                nc.scalar.activation(EB[:, :, :], Z2[:, 2 * j:2 * j + 2, :], ACT.Exp).then_inc(b_exp, 1)

            def sq2(s):
                act.wait_ge(b_cut, s + 1)
                nc.scalar.activation(EB[:, :, :], EB[:, :, :], ACT.Square).then_inc(b_sq, 1)

            def log2(s):
                act.wait_ge(b_sq, s + 1)
                nc.scalar.activation(EB[:, :, :], EB[:, :, :], ACT.Ln, bias=CONST[:, 0:1]).then_inc(b_ln, 1)

            def inv2(s):
                act.wait_ge(b_ln, s + 1)
                nc.scalar.activation(EB[:, :, :], EB[:, :, :], ACT.Exp, scale=-1.0).then_inc(b_r, 1)

            def attr_high(i, j):
                s = 2 * i + j
                act.wait_ge(attr_in[j], 16 * (i + 1))
                if not isinstance(s, int) or s >= 2:
                    act.wait_ge(z1_done[1], s - 1)
                nc.scalar.copy(AT_R[:, j, :], AT_RAW[:, j, :]).then_inc(attr_hi, 1)

            def mish_a(s, j):
                for h in range(2):
                    exp1(s, h)
                for h in range(2):
                    log1(s, h)
                for h in range(2):
                    inv1(s, h)
                for h in range(2):
                    hi1(s, j, h)

            def mish_b(s, j):
                exp2(s, j)
                sq2(s)
                log2(s)
                inv2(s)

            def edge_step(i, j, more):
                s = 2 * i + j
                exp2(s - 2, j)
                sq2(s - 2)
                exp1(s, 0)
                log2(s - 2)
                exp1(s, 1)
                if more:
                    attr_high(i + j, 1 - j)
                inv2(s - 2)
                for step in (log1, inv1):
                    for h in range(2):
                        step(s, h)
                for h in range(2):
                    hi1(s, j, h)

            for j in range(2):
                attr_high(0, j)
            mish_a(0, 0)
            attr_high(1, 0)
            mish_a(1, 1)
            with act.Fori(1, PAIRS // 2 - 1) as i:
                for j in range(2):
                    edge_step(i, j, True)
            for j in range(2):
                edge_step(PAIRS // 2 - 1, j, j == 0)
            mish_b(PAIRS - 2, 0)
            mish_b(PAIRS - 1, 1)

            move_t(AT2, scale=-2.0)
            move_t(T1)
            with act.Fori(0, BLOCKS) as b:
                for o in range(KD):
                    n = KD * b + o
                    act.wait_ge(mm_done, MM_PQ + 2 * NT + n + 1)
                    nc.scalar.activation(UT[:, o, bass.ds(b * BW, BW)], Z2[:, o, 0:BW], ACT.Identity,
                                         bias=COLS[:, CB3 + o:CB3 + o + 1]).then_inc(u_bias, 1)
                    act.wait_ge(u_cut, n + 1)
                    nc.scalar.activation(XWORK, XWORK, ACT.Exp).then_inc(u_exp, 1)
                    act.wait_ge(u_exp, n + 1)
                    nc.scalar.activation(XWORK, XWORK, ACT.Square, bias=CONST[:, 0:1]).then_inc(u_sq, 1)
                    act.wait_ge(u_sq, n + 1)
                    nc.scalar.activation(XWORK, XWORK, ACT.Ln, bias=CONST[:, 0:1]).then_inc(u_ln, 1)
                    act.wait_ge(u_ln, n + 1)
                    nc.scalar.activation(XWORK, XWORK, ACT.Exp, scale=-1.0).then_inc(u_r, 1)
            std(NT, VAR[:, :], 5)

        @block.vector
        def _(dve):
            chain = [0]

            def link(ins):
                chain[0] += 1
                ins.then_inc(dve_chain, 1)
                dve.wait_ge(dve_chain, chain[0])

            extras = dve.alloc_register("dve_extras")
            dve.reg_mov(extras, 1)

            def ln_stats(source):
                base = chain[0]
                with dve.Fori(0, NT) as nt:
                    nc.vector.bn_stats(STATS[:, bass.ds(nt, 1), :].rearrange("p o s -> p (o s)"),
                                       source[:, bass.ds(nt, 1), :].rearrange("p o d -> p (o d)")).then_inc(dve_chain, 1)
                chain[0] += NT
                dve.wait_ge(dve_chain, chain[0])
                even, odd = STATS[:, :, 1], STATS[:, :, 4]
                nc.vector.tensor_tensor(TMP[:, 0, :], even, odd, ALU.add).then_inc(dve_chain, 1)
                nc.vector.tensor_tensor(TMP[:, 1, :], even, odd, ALU.subtract).then_inc(dve_chain, 1)
                nc.vector.tensor_tensor(TMP[:, 2, :], STATS[:, :, 2], STATS[:, :, 5], ALU.add).then_inc(dve_chain, 1)
                chain[0] += 3
                dve.wait_ge(dve_chain, chain[0])
                nc.vector.tensor_scalar(MEAN[:, :], TMP[:, 0, :], 0.5, None, ALU.mult).then_inc(dve_chain, 1)
                nc.vector.scalar_tensor_tensor(TMP[:, 4, :], TMP[:, 1, :], 0.25, TMP[:, 1, :], ALU.mult, ALU.mult).then_inc(dve_chain, 1)
                chain[0] += 2
                dve.wait_ge(dve_chain, chain[0])
                nc.vector.scalar_tensor_tensor(VAR[:, :], TMP[:, 2, :], 1.0 / DIM, TMP[:, 4, :], ALU.mult, ALU.add).then_inc(var_ready, 1)

            def ln_rstd(count):
                dve.wait_ge(std_ready, count)
                link(nc.vector.reciprocal(RSTD[:, :], TMP[:, 3, :]))

            def normalise(target, source):
                with dve.Fori(0, NT) as nt:
                    nc.vector.tensor_scalar(target[:, bass.ds(nt, 1), :].rearrange("p o d -> p (o d)"),
                                            source[:, bass.ds(nt, 1), :].rearrange("p o d -> p (o d)"),
                                            MEAN[:, bass.ds(nt, 1)], RSTD[:, bass.ds(nt, 1)],
                                            ALU.subtract, ALU.mult).then_inc(dve_chain, 1)
                chain[0] += NT
                dve.wait_ge(dve_chain, chain[0])

            def batch_norm(source, on, gamma, beta, var_count, std_count):
                for o in range(on):
                    for k, (a, b) in enumerate(BN_PIECES):
                        ins = nc.vector.bn_stats(BSTATS[:, o, 6 * k:6 * k + 6], source[:, o, a:b])
                        ins.then_inc(dve_chain, 1)
                        chain[0] += 1
                dve.wait_ge(dve_chain, chain[0])
                for o in range(on):
                    ins = nc.vector.bn_aggr(MV[:, o, :], BSTATS[:, o, :])
                    ins.then_inc(dve_chain, 1) if o < on - 1 else ins.then_inc(var_ready, 1)
                    chain[0] += o < on - 1
                dve.wait_ge(dve_chain, chain[0])
                dve.wait_ge(var_ready, var_count)
                dve.wait_ge(std_ready, std_count)
                link(nc.vector.reciprocal(TMP[:, 0, 0:on], TMP[:, 3, 0:on]))
                link(nc.vector.tensor_tensor(SCALE[:, 0:on], TMP[:, 0, 0:on], COLS[:, gamma:gamma + on], ALU.mult))
                link(nc.vector.tensor_tensor(TMP[:, 1, 0:on], MV[:, 0:on, 0], SCALE[:, 0:on], ALU.mult))
                nc.vector.tensor_tensor(SHIFT[:, 0:on], COLS[:, beta:beta + on], TMP[:, 1, 0:on], ALU.subtract).then_inc(bn_ready, 1)

            low_regs = [[dve.alloc_register(f"dve_low{n}_{j}") for j in range(R_EXTRA + 1)] for n in range(4)]

            def load_range(n, s):
                dve.load(low_regs[n], pair_range(s, R_LOW, R_EXTRA + 1))

            def low_tile(n, j):
                return dve.snap(low_regs[n][j], min_val=0, max_val=NT - 1)

            def hot(at, tile, low):
                nc.vector.tensor_scalar(at, IOTA[:, bass.ds(low * P, P)], DSTF[:, bass.ds(tile, 1)], None,
                                        ALU.is_equal).then_inc(hot_ready, 1)

            def add_sums(low, bank):
                a = AGG[:, bass.ds(low, 1), :].rearrange("p o d -> p (o d)")
                nc.vector.tensor_tensor(a, a, bank, ALU.add).then_inc(agg_done, 1)

            def sums_extra(s, j, bank, added):
                low = dve.value_load(pair_range(s, R_LOW + j, 1), min_val=0, max_val=NT - 1)
                high = dve.value_load(pair_range(s, R_HIGH + j, 1), min_val=0, max_val=NT - 1)
                with dve.If(low < high):
                    with dve.Fori(low + 1, high + 1) as nt:
                        n = dve.snap(extras)
                        dve.wait_ge(agg_done, added)
                        dve.wait_ge(xseg_done, n)
                        dve.wait_ge(xagg_done, n)
                        nc.vector.tensor_scalar(XHOT[:, :], IOTA[:, bass.ds(nt * P, P)], DSTF[:, bass.ds(2 * s + j, 1)],
                                                None, ALU.is_equal).then_inc(xhot_ready, 1)
                        dve.wait_ge(xseg_done, n + 1)
                        a = AGG[:, bass.ds(nt, 1), :].rearrange("p o d -> p (o d)")
                        nc.vector.tensor_tensor(a, a, bank, ALU.add).then_inc(xagg_done, 1)
                        dve.reg_add(extras, extras, 1)

            nc.vector.memset(CONST[:, 0:1], 1.0).then_inc(dve_chain, 1)
            nc.vector.memset(B2_R[:, :].bitcast(F32), 0.0).then_inc(dve_chain, 1)
            nc.vector.memset(ONES_R[:, :].bitcast(F32), 1.0).then_inc(dve_chain, 1)
            chain[0] += 3
            nc.vector.memset(AGG[:, :, :], 0.0).then_inc(agg_done, 1)
            for n, (start, count) in enumerate(((mm_moved, FREE), (u_ready, KD), (msg_ready, 1),
                                                (xhot_ready, 1), (xseg_done, 1), (xagg_done, 1))):
                nc.vector.memset(TMP[:, 0, n:n + 1], 0.0).then_inc(start, count)
            nc.vector.memset(CONST[:, 1:2], LN_EPS).then_inc(dve_const, 1)
            link(nc.vector.memset(RNG_T[:, :], 0))
            dve.wait_ge(idx_in, 48)
            nc.vector.tensor_copy(DSTF[:, :], DST[:, :]).then_inc(dve_chain, 1)
            low, high, past = RNG_T[:, R_LOW:R_LOW + 2], RNG_T[:, R_HIGH:R_HIGH + 2], RNG_T[:, R_EXTRA:R_EXTRA + 2]
            nc.vector.tensor_reduce(low, DROW[:, :, :], AX.X, ALU.min).then_inc(dve_chain, 1)
            nc.vector.tensor_reduce(high, DROW[:, :, :], AX.X, ALU.max).then_inc(dve_chain, 1)
            chain[0] += 3
            dve.wait_ge(dve_chain, chain[0])
            link(nc.vector.tensor_scalar(RNG_T[:, :], RNG_T[:, :], P.bit_length() - 1, None, ALU.arith_shift_right))
            link(nc.vector.tensor_tensor(past, high, low, ALU.subtract))
            nc.vector.tensor_tensor(past[:, 0:1], past[:, 0:1], past[:, 1:2], ALU.add).then_inc(range_ready, 1)
            dve.wait_ge(x_in, 16)
            ln_stats(X)
            ln_rstd(1)
            normalise(H, X)
            nc.vector.tensor_scalar(H[:, :, :], H[:, :, :], 0.0, None, ALU.max).then_inc(h_ready, 1)
            dve.wait_ge(split_in, 48)
            dve.wait_ge(small_in, 48)
            link(nc.vector.tensor_scalar(W2_RAW[:, :, :], W2_RAW[:, :, :], -2.0, None, ALU.mult))
            nc.vector.tensor_copy(W2_HI[:, :, :], W2_RAW[:, :, :]).then_inc(dve_chain, 1)
            nc.vector.tensor_copy(WE_HI[:, :], WE_RAW[:, :]).then_inc(dve_chain, 1)
            nc.vector.tensor_copy(B2_R[0:1, :], ROWS[0:1, ROW_B2, :]).then_inc(dve_chain, 1)
            nc.vector.tensor_copy(B2_R[32:33, :], ROWS[32:33, ROW_B2, :]).then_inc(dve_chain, 1)
            nc.vector.tensor_scalar(EPS1[:, :], EPS1[:, :], 1.0, None, ALU.add).then_inc(dve_chain, 1)
            chain[0] += 5
            dve.wait_ge(dve_chain, chain[0])
            nc.vector.tensor_tensor(W2_LO[:, :, :], W2_RAW[:, :, :], W2_HI[:, :, :].bitcast(F32), ALU.subtract).then_inc(dve_chain, 1)
            nc.vector.tensor_tensor(WE_LO[:, :], WE_RAW[:, :], WE_HI[:, :].bitcast(F32), ALU.subtract).then_inc(dve_chain, 1)
            nc.vector.tensor_tensor(B2_R[32:33, :], ROWS[32:33, ROW_B2, :], B2_R[32:33, :].bitcast(F32), ALU.subtract).then_inc(dve_chain, 1)
            chain[0] += 3
            dve.wait_ge(dve_chain, chain[0])

            dve.wait_ge(pool_const, 3)
            dve.wait_ge(range_in, 16)

            def hots0(n, half):
                for k in range(2):
                    load_range(2 * half + k, 2 * n + k)
                for j in range(GROUP):
                    hot(HOT0[:, half, j, :], GROUP * n + j, low_tile(2 * half + j // 2, j % 2))

            def sums0(n, half):
                def add(j):
                    dve.wait_ge(agg_done, SUMS0 + GROUP * n + j)
                    add_sums(low_tile(2 * half + j // 2, j % 2), BANKS[:, GROUP * half + j, :])
                dve.wait_ge(seg_done, GROUP * (n + 1))
                for j in range(GROUP - 1):
                    add(j)
                past = [dve.snap(low_regs[2 * half + k][R_EXTRA]) for k in range(2)]
                with dve.If(past[0] + past[1] > 0):
                    for j in range(GROUP):
                        sums_extra(2 * n + j // 2, j % 2, BANKS[:, GROUP * half, :], SUMS0 + GROUP * (n + 1) - 1)
                    extra = dve.snap(extras)
                    dve.wait_ge(xagg_done, extra)
                    nc.vector.memset(XHOT[:, 0:1], 0.0)
                add(GROUP - 1)

            hots0(0, 0)
            def groups0(i, last):
                for g in range(RING):
                    n = RING * i + g
                    if not last or g < RING - 1:
                        hots0(n + 1, (g + 1) % 2)
                    sums0(n, g % 2)

            with dve.Fori(0, GROUPS // RING - 1) as i:
                groups0(i, False)
            groups0(GROUPS // RING - 1, True)
            dve.wait_ge(agg_done, SUMS0 + TILES)
            nc.vector.scalar_tensor_tensor(AGG[:, :, :].rearrange("p t d -> p (t d)"), H[:, :, :].rearrange("p t d -> p (t d)"),
                                           EPS1[:, 0:1], AGG[:, :, :].rearrange("p t d -> p (t d)"),
                                           ALU.mult, ALU.add).then_inc(z0_ready, 1)
            link(nc.vector.tensor_tensor(X[:, :, :], X[:, :, :], H[:, :, :], ALU.add))
            dve.wait_ge(mm_moved, FREE + MM_2)
            batch_norm(H1T, KH, CG1, CBE1, 2, 2)
            dve.wait_ge(mm_moved, FREE + MM_PQ)
            batch_norm(T1, KD, CG2, CBE2, 3, 3)
            for nt in range(NT):
                dve.wait_ge(tr_done, TR_R2 + nt + 1)
                nc.vector.tensor_tensor(X[:, nt, :], X[:, nt, :], SEG[:, (TR_R2 + nt) % 2, :], ALU.add).then_inc(tr_moved, 1)
            dve.wait_ge(tr_moved, TR_R2 + NT)
            ln_stats(X)
            ln_rstd(4)
            dve.wait_ge(h_stored, 16)
            normalise(H, X)
            nc.vector.tensor_scalar(H[:, :, :], H[:, :, :], 0.0, None, ALU.max).then_inc(h_ready, 1)
            for nt in range(NT):
                dve.wait_ge(mm_done, MM_PQ + 2 * nt + 2)
                nc.vector.tensor_tensor(QST[:, nt, :], Z2[:, 2 + nt % 2, :], ROWS[:, ROW_B1, :], ALU.add).then_inc(q_moved, 1)
            dve.wait_ge(pq_stored, 32)
            nc.vector.memset(AGG[:, :, :], 0.0).then_inc(agg_done, 1)

            def attr_rest(s, j):
                dve.wait_ge(attr_hi, s + 1)
                low = AT_R[EDGE_DIM:P, j, :]
                nc.vector.tensor_tensor(low, AT_RAW[EDGE_DIM:P, j, :], low.bitcast(F32), ALU.subtract).then_inc(attr_ready, 1)

            def cut1(s, h):
                dve.wait_ge(a_exp[h], s + 1)
                at = EA[:, 2 * h:2 * h + 2, :]
                nc.vector.tensor_scalar(at, at, E_MAX, 1.0, ALU.min, ALU.add).then_inc(a_cut[h], 1)

            def sq1(s, h):
                dve.wait_ge(a_cut[h], s + 1)
                at = EA[:, 2 * h:2 * h + 2, :]
                nc.vector.tensor_tensor(at, at, at, ALU.mult).then_inc(a_sq[h], 1)

            def full1(s, h):
                dve.wait_ge(a_r[h], s + 1)
                if not (isinstance(s, int) and s == 0):
                    dve.wait_ge(h_lo[h], s)
                nc.vector.scalar_tensor_tensor(HF[:, 2 * h:2 * h + 2, :].rearrange("p c e -> p (c e)"),
                                               EA[:, 2 * h:2 * h + 2, :].rearrange("p c e -> p (c e)"),
                                               -0.5, Z1[:, h, :], ALU.add, ALU.mult).then_inc(h_full[h], 1)

            def lo1(s, j, h):
                dve.wait_ge(h_hi[h], s + 1)
                c = slice(2 * h, 2 * h + 2)
                nc.vector.tensor_tensor(H_LO[:, j, c, :], HF[:, c, :], H_HI[:, j, c, :].bitcast(F32), ALU.subtract).then_inc(h_lo[h], 1)

            def cut2(s):
                dve.wait_ge(b_exp, s + 1)
                nc.vector.tensor_scalar(EB[:, :, :], EB[:, :, :], E_MAX, 1.0, ALU.min, ALU.add).then_inc(b_cut, 1)

            def hots1(s):
                for k in range(2):
                    hot(ONEHOT[:, k, :], 2 * s + k, low_tile(0, k))

            def message(s, j):
                dve.wait_ge(b_r, s + 1)
                nc.vector.scalar_tensor_tensor(MSG[:, :, :].rearrange("p k d -> p (k d)"), EB[:, :, :].rearrange("p k d -> p (k d)"),
                                               -0.5, Z2[:, 2 * j:2 * j + 2, :].rearrange("p k d -> p (k d)"),
                                               ALU.add, ALU.mult).then_inc(msg_ready, 1)

            def sums1(s):
                dve.wait_ge(seg_done, TILES + 2 * (s + 1))
                for j in range(2):
                    dve.wait_ge(agg_done, SUMS1 + 2 * s + j)
                    add_sums(low_tile(0, j), SEG[:, j, :])
                past = dve.snap(low_regs[0][R_EXTRA])
                with dve.If(past > 0):
                    for j in range(2):
                        sums_extra(s, j, SEG[:, 0, :], SUMS1 + 2 * (s + 1))
                    extra = dve.snap(extras)
                    dve.wait_ge(xagg_done, extra)
                    nc.vector.memset(XHOT[:, 0:1], 0.0)

            def mish_a(s, j):
                for step in (cut1, sq1, full1):
                    for h in range(2):
                        step(s, h)
                for h in range(2):
                    lo1(s, j, h)

            def mish_b(s, j):
                load_range(0, s)
                cut2(s)
                hots1(s)
                message(s, j)
                sums1(s)

            def edge_step(s, j, more):
                load_range(0, s - 2)
                cut2(s - 2)
                hots1(s - 2)
                for h in range(2):
                    cut1(s, h)
                    sq1(s, h)
                if more:
                    attr_rest(s + 1, 1 - j)
                message(s - 2, j)
                for h in range(2):
                    full1(s, h)
                for h in range(2):
                    lo1(s, j, h)
                sums1(s - 2)

            for j in range(2):
                attr_rest(j, j)
            mish_a(0, 0)
            attr_rest(2, 0)
            mish_a(1, 1)
            with dve.Fori(1, PAIRS // 2 - 1) as i:
                for j in range(2):
                    edge_step(2 * i + j, j, True)
            for j in range(2):
                edge_step(PAIRS - 2 + j, j, j == 0)
            mish_b(PAIRS - 2, 0)
            mish_b(PAIRS - 1, 1)
            dve.wait_ge(agg_done, SUMS1 + TILES)

            with dve.Fori(0, BLOCKS) as b:
                for o in range(KD):
                    n = KD * b + o
                    at = UT[:, o, bass.ds(b * BW, BW)]
                    dve.wait_ge(u_bias, n + 1)
                    dve.wait_ge(u_ready, KD + n)
                    nc.vector.tensor_scalar(XWORK, at, Z_MAX, None, ALU.min).then_inc(u_cut, 1)
                    dve.wait_ge(u_r, n + 1)
                    nc.vector.scalar_tensor_tensor(at, XWORK, -0.5, at, ALU.add, ALU.mult).then_inc(u_ready, 1)
            def wide(row):
                return ROWS[:, row:row + 1, :].broadcast_to([P, NT, DIM])
            dve.wait_ge(tr_moved, 5 * NT)
            link(nc.vector.tensor_tensor(H[:, :, :], H[:, :, :], wide(ROW_B4), ALU.add))
            link(nc.vector.tensor_tensor(X[:, :, :], X[:, :, :], wide(ROW_BETA), ALU.add))
            for nt in range(NT):
                dve.wait_ge(y_done, nt + 1)
                nc.vector.scalar_tensor_tensor(AGG[:, nt, :], Z2[:, nt % 2, :], -2.0, H[:, nt, :], ALU.mult, ALU.add).then_inc(y_moved, 1)
            dve.wait_ge(y_moved, NT)
            ln_stats(AGG)
            ln_rstd(5)
            normalise(AGG, AGG)
            link(nc.vector.tensor_tensor(AGG[:, :, :], AGG[:, :, :], wide(ROW_GAMMA), ALU.mult))
            for nt in range(NT):
                nc.vector.tensor_tensor(H[:, nt, :], AGG[:, nt, :], X[:, nt, :], ALU.add).then_inc(out_ready, 1)


def kernel(**inputs):
    import numpy as np
    import concourse.bacc as bacc
    from concourse.bass_utils import run_bass_kernel_spmd

    get = lambda name: np.asarray(inputs[name])
    x = np.zeros((NP, DIM), np.float32)
    x[:NODES] = get("x")
    src = np.zeros(TILES * P, np.int32)
    src[:EDGES] = get("src")
    dst = np.full(TILES * P, NP - 1, np.int32)
    dst[:EDGES] = get("dst")
    attr = np.zeros((TILES * P, EDGE_DIM), np.float32)
    attr[:EDGES] = get("edge_attr_64")
    attr = attr.reshape(PAIRS, PW, EDGE_DIM).transpose(0, 2, 1)
    columns = ["L0_gnn_b1", "L0_gnn_g1", "L0_gnn_be1", "L0_gnn_b2", "L0_gnn_g2", "L0_gnn_be2", "L1_gnn_b3"]
    rows = ["L1_gnn_b1", "L1_gnn_b2", "L1_gnn_b4", "L1_gnn_gamma", "L1_gnn_beta"]
    arrays = {
        "x": x,
        "src_cols": src.reshape(TILES, P).T,
        "dst_cols": dst.reshape(TILES, P).T,
        "dst_rows": dst.reshape(PAIRS, 2, P),
        "edge_attr_t": np.concatenate([attr, attr], axis=1),
        "eps": get("L0_gnn_eps").reshape(1),
        "cols": np.concatenate([get(n).reshape(-1, P).T for n in columns], axis=1),
        "rows": np.stack([get(n) for n in rows]),
        "w01": get("L0_gnn_W1"), "w02": get("L0_gnn_W2"),
        "w1": get("L1_gnn_W1"), "w2": get("L1_gnn_W2"), "w3": get("L1_gnn_W3"), "w4": get("L1_gnn_W4"),
    }
    nc = bacc.Bacc("TRN2", target_bir_lowering=False, num_devices=1)
    feeds, args = {}, {}
    for name, a in arrays.items():
        a = np.ascontiguousarray(a)
        feeds[f"in_{name}"] = a
        args[name] = nc.dram_tensor(f"in_{name}", a.shape, mybir.dt.from_np(a.dtype), kind="ExternalInput").ap()
    args["out"] = nc.dram_tensor("out_x", (NODES, DIM), F32, kind="ExternalOutput").ap()
    gnn_kernel(nc, **args)
    r = run_bass_kernel_spmd(nc, [feeds], core_ids=[0])
    return r.results[0]["out_x"]
```

```python
from contextlib import ExitStack

import concourse.bass as bass
from concourse import mybir

ALU = mybir.AluOpType
ACT = mybir.ActivationFunctionType
F32 = mybir.dt.float32
F32R = mybir.dt.float32r
I32 = mybir.dt.int32
AX = mybir.AxisListType

P = 128
NODES, DIM, HID0, EDGE_DIM = 1250, 512, 1024, 64
EDGES = 20000
NT = -(-NODES // P)
NP = NT * P
KD = DIM // P
KH = HID0 // P
GROUP = 4
RING = 4
TILES = -(-EDGES // (GROUP * RING * P)) * GROUP * RING
GROUPS = TILES // GROUP
PAIRS = TILES // 2
R_LOW, R_EXTRA, R_FIRST, R_WORK, R_WORDS = 0, 2, 3, 4, 8
R_USED = 4
SIGN_BIT = 5
assert 2 * NT < 1 << SIGN_BIT
PW = 2 * P
SLOTS = 4
BLOCKS = 4
BW = NP // BLOCKS
LN_EPS = BN_EPS = 1e-5
E_MAX = 1e9
Z_MAX = 20.0
BN_PIECES = [(b * BW, min((b + 1) * BW, NODES)) for b in range(BLOCKS)]
LN_GROUPS = [(a, min(a + 3, NT)) for a in range(0, NT, 3)]
LG = len(LN_GROUPS)
CB1, CG1, CBE1, CB2, CG2, CBE2, CB3 = 0, 8, 16, 24, 28, 32, 36
NCOLS = 40
ROW_B1, ROW_B2, ROW_B4, ROW_GAMMA, ROW_BETA = range(5)


def gnn_kernel(nc, x, src_cols, dst_cols, dst_rows, edge_attr_t, eps, cols, rows, w01, w02,
               w1, w2, w3, w4, out):
    ctx = ExitStack()
    with ctx:
        place = [nc.sbuf_base + (-nc.sbuf_base) % 64]

        def sb(name, shape, dt=F32, at=None):
            size = 4
            for n in shape[1:]:
                size *= n
            if at is None:
                at = place[0]
                place[0] += size + (-size) % 32
            return nc.alloc_sbuf_tensor_at(name, shape, dt, offset=at), at + size + (-size) % 32

        X, _ = sb("x_nodes", [P, NT, DIM])
        H, _ = sb("h_nodes", [P, NT, DIM])
        AGG, _ = sb("agg_nodes", [P, NT, DIM])
        t1_at = place[0]
        T1, _ = sb("act_t", [P, KD, NP])
        h1t_at = place[0]
        H1T, _ = sb("hidden_t", [P, KH, NP])
        WA, _ = sb("weights_a", [P, 2 * KD, DIM])
        WB, _ = sb("weights_b", [P, 2 * KD, DIM])
        WA0 = WA[:, :, :].rearrange("p (k h) n -> p k (h n)", k=KD)
        W4 = WA[:, 0:KD, :]
        XWORK = WA[:, KD, 0:BW]
        W2_HI, _ = sb("w2_hi", [P, KD, DIM], F32R)
        W2_LO, _ = sb("w2_lo", [P, KD, DIM], F32R)
        WE_HI, _ = sb("we_hi", [P, DIM], F32R)
        WE_LO, _ = sb("we_lo", [P, DIM], F32R)
        B2_R, _ = sb("b2_parts", [64, DIM], F32R)
        ONES_R, _ = sb("ones", [64, P], F32R)
        ROWS, _ = sb("rows", [P, 5, DIM])
        IOTA, _ = sb("iota", [P, NP])
        IDENT, _ = sb("ident", [P, P])
        SRC, _ = sb("src", [P, TILES], I32)
        DST, _ = sb("dst", [P, TILES], I32)
        DSTF, _ = sb("dst_f", [P, TILES])
        RANGE, _ = sb("tile_range", [1, R_WORDS * PAIRS], I32)
        IDX, _ = sb("gather_index", [P, RING, 4], I32)
        ONEHOT, _ = sb("onehot", [P, 2, P])
        XHOT, _ = sb("onehot_extra", [P, P])
        COLS, _ = sb("cols", [P, NCOLS])
        STATS, _ = sb("stats", [P, NT, 6])
        BSTATS, _ = sb("bn_stats", [P, KH, 6 * BLOCKS])
        MV, _ = sb("bn_mean_var", [P, KH, 2])
        LN_MV, _ = sb("ln_mean_var", [P, NT, 2])
        NBIAS, _ = sb("ln_bias", [P, NT])
        RSTD, _ = sb("rstd", [P, NT])
        TMP, _ = sb("tmp", [P, 5, NT])
        SCALE, _ = sb("bn_scale", [P, KH])
        SHIFT, _ = sb("bn_shift", [P, KH])
        EPS1, _ = sb("eps1", [P, 1])
        CONST, _ = sb("consts", [P, 2])
        assert place[0] <= nc.sbuf_usable_end, place[0] - nc.sbuf_usable_end
        ROWS0, at = sb("gather_h", [P, RING, GROUP, DIM], at=t1_at)
        HOT0, at = sb("onehot_0", [P, RING, GROUP, P], at=at)
        DROW, at = sb("dst_tiles", [PAIRS, 2, P], I32, at=at)
        RNG_T, at = sb("range_tiles", [PAIRS, R_WORDS], I32, at=at)
        assert at <= h1t_at + 4 * KH * NP
        W2_RAW, WE_RAW = AGG[:, 0:KD, :], AGG[:, KD, :]
        QST, _ = sb("q_stage", [P, NT, DIM], at=h1t_at)
        EA, at = sb("mish1_work", [P, KD, PW], at=t1_at)
        EB, at = sb("mish2_work", [P, 2, DIM], at=at)
        HF, at = sb("h_full", [P, KD, PW], at=at)
        GP, at = sb("gather_pq", [P, 2 * SLOTS, DIM], at=at)
        H_HI, at = sb("h_hi", [P, 2, KD, PW], F32R, at=at)
        H_LO, at = sb("h_lo", [P, 2, KD, PW], F32R, at=at)
        MSG, at = sb("message", [P, 2, DIM], at=at)
        AT_RAW, at = sb("edge_attr", [P, 2, PW], at=at)
        AT_R, at = sb("edge_attr_parts", [P, 2, PW], F32R, at=at)
        assert at <= h1t_at + 4 * KH * NP
        AT2, _ = sb("agg_t", [P, KD, NP], at=h1t_at)
        UT, _ = sb("u_t", [P, KD, NP], at=h1t_at + 4 * KD * NP)

        BANKS = ctx.enter_context(nc.psum_tensor("banks", [P, 8, 512], F32))
        Z1, SEG, Z2 = BANKS[:, 0:2, :], BANKS[:, 2:4, :], BANKS[:, 4:8, :]
        Z1v = Z1[:, :, :].rearrange("p b (c e) -> p (b c) e", c=2)

        h_tab = nc.dram_tensor("h_table", [NP, DIM], F32)
        p_tab = nc.dram_tensor("p_table", [NP, DIM], F32)
        q_tab = nc.dram_tensor("q_table", [NP, DIM], F32)
        r_tab = nc.dram_tensor("range_table", [PAIRS, R_WORDS], I32)

        def sem(name):
            return ctx.enter_context(nc.semaphore(name))

        idx_in, small_in, w01_in, w02_in = (sem(n) for n in ("idx_in", "small_in", "w01_in", "w02_in"))
        x_in = [sem(f"x_in{g}") for g in range(LG)]
        split_in, w1_in, w3_in, w4_in = (sem(n) for n in ("split_in", "w1_in", "w3_in", "w4_in"))
        range_out, range_in, range_ready = (sem(n) for n in ("range_out", "range_in", "range_ready"))
        pool_const, dve_const, dve_chain = (sem(n) for n in ("pool_const", "dve_const", "dve_chain"))
        var_ready, std_ready, h_ready, h_stored = (sem(n) for n in
            ("var_ready", "std_ready", "h_ready", "h_stored"))
        norm_done, scale_ready, drow_in, r2_moved, rows_in = (sem(n) for n in
            ("norm_done", "scale_ready", "drow_in", "r2_moved", "rows_in"))
        idx_copied = sem("idx_copied")
        gat0 = [sem(f"gathered0_{g}") for g in range(RING)]
        gat1 = [sem(f"gathered1_{j}") for j in range(SLOTS)]
        hot_ready, seg_done, agg_done = sem("hot_ready"), sem("seg_done"), sem("agg_done")
        xhot_ready, xseg_done, xagg_done = sem("xhot_ready"), sem("xseg_done"), sem("xagg_done")
        z0_ready = sem("z0_ready")
        tr_done, tr_moved = sem("tr_done"), sem("tr_moved")
        mm_done, mm_moved = sem("mm_done"), sem("mm_moved")
        bn_ready, bn_applied = sem("bn_ready"), sem("bn_applied")
        q_moved, pq_stored = sem("q_moved"), sem("pq_stored")
        attr_in = [sem(f"attr_in{j}") for j in range(2)]
        attr_hi, attr_ready = sem("attr_hi"), sem("attr_ready")
        z1_done, a_exp, a_cut, a_sq, a_ln, a_r, h_full, h_hi, h_lo = ([sem(f"{n}_{h}") for h in range(2)] for n in
            ("z1_done", "a_exp", "a_cut", "a_sq", "a_ln", "a_r", "h_full", "h_hi", "h_lo"))
        z2_done = sem("z2_done")
        b_exp, b_cut, b_sq, b_ln, b_r, msg_ready = (sem(n) for n in
            ("b_exp", "b_cut", "b_sq", "b_ln", "b_r", "msg_ready"))
        u_bias, u_exp, u_cut, u_sq, u_ln, u_r, u_ready = (sem(n) for n in
            ("u_bias", "u_exp", "u_cut", "u_sq", "u_ln", "u_r", "u_ready"))
        y_done, y_moved, out_ready, out_stored = (sem(n) for n in
            ("y_done", "y_moved", "out_ready", "out_stored"))

        block = ctx.enter_context(nc.Block())

        def pair_range(s, word, n):
            return RANGE[0:1, bass.ds(R_WORDS * s + word, n)]

        TR_R2 = NT
        MOVED_H2, MOVED_AGG, MOVED_H3 = (NT * n for n in (1, 2, 3))
        SUMS0, SUMS1 = 1, TILES + 2
        MM_1 = 0
        FREE = 4
        MM_2 = BLOCKS * KH
        MM_PQ = MM_2 + BLOCKS * KD
        H_STORED, PQ_STORED = 16 * LG, 16 * 2 * NT

        @block.sync
        def _(sp):
            sp.dma_start(DROW[:, :, :], dst_rows).then_inc(drow_in, 16)
            for g, (a, b) in enumerate(LN_GROUPS):
                sp.dma_start(X[:, a:b, :], x[a * P:b * P, :].rearrange("(t p) d -> p t d", p=P)).then_inc(x_in[g], 16)
            sp.dma_start(SRC[:, :], src_cols).then_inc(idx_in, 16)
            sp.dma_start(DST[:, :], dst_cols).then_inc(idx_in, 16)
            sp.dma_start(COLS[:, :], cols).then_inc(small_in, 16)
            sp.dma_start(EPS1[:, :], eps.partition_broadcast(P)).then_inc(small_in, 16)
            sp.wait_ge(range_ready, 2)
            sp.dma_start(r_tab[:, :], RNG_T[:, :]).then_inc(range_out, 16)
            sp.wait_ge(range_out, 16)
            sp.dma_start(RANGE[0:1, :], r_tab.rearrange("(o s) j -> o (s j)", o=1)).then_inc(range_in, 16)
            for a, b in LN_GROUPS:
                sp.wait_ge(h_ready, b)
                sp.dma_start(h_tab[a * P:b * P, :].rearrange("(t p) d -> p t d", p=P), H[:, a:b, :]).then_inc(h_stored, 16)
            for c in range(KD):
                sp.wait_ge(agg_done, SUMS0 + GROUP * (RING + 2 * c))
                sp.dma_start(WA0[:, c, :], w01[c * P:(c + 1) * P, :]).then_inc(w01_in, 16)
            for c in range(KD):
                sp.wait_ge(agg_done, SUMS0 + GROUP * (RING + 2 * (KD + c)))
                sp.dma_start(WB[:, 2 * c:2 * c + 2, :], w02[2 * c * P:2 * (c + 1) * P, :].rearrange("(k p) n -> p k n", p=P)).then_inc(w02_in, 16)
            sp.wait_ge(agg_done, SUMS0 + GROUP * (RING + 4 * KD))
            sp.dma_start(ROWS[:, :, :], rows.partition_broadcast(P)).then_inc(rows_in, 16)
            sp.wait_ge(tr_done, NT)
            sp.dma_start(W2_RAW, w2.rearrange("(k p) n -> p k n", p=P)).then_inc(split_in, 16)
            for half in range(2):
                sp.dma_start(WE_RAW[EDGE_DIM * half:EDGE_DIM * (half + 1), :], w1[2 * DIM:, :]).then_inc(split_in, 16)
            sp.wait_ge(mm_done, MM_2)
            sp.dma_start(WA[:, :, :], w1[0:2 * DIM, :].rearrange("(k p) n -> p k n", p=P)).then_inc(w1_in, 16)
            sp.wait_ge(mm_done, MM_PQ)
            sp.dma_start(WB[:, :, :], w3.rearrange("(k p) n -> p k n", p=P)).then_inc(w3_in, 16)
            for nt in range(NT):
                sp.wait_ge(mm_moved, FREE + MM_PQ + nt + 1)
                sp.dma_start(p_tab[nt * P:(nt + 1) * P, :], AGG[:, nt, :]).then_inc(pq_stored, 16)
                sp.wait_ge(q_moved, nt + 1)
                sp.dma_start(q_tab[nt * P:(nt + 1) * P, :], QST[:, nt, :]).then_inc(pq_stored, 16)
            sp.dma_start(W4, w4.rearrange("(k p) n -> p k n", p=P)).then_inc(w4_in, 16)
            sp.wait_ge(pq_stored, PQ_STORED)
            for j in range(2):
                sp.dma_start(AT_RAW[:, j, :], edge_attr_t[j, :, :]).then_inc(attr_in[j], 16)
            with sp.Fori(1, PAIRS // 2) as i:
                for j in range(2):
                    sp.wait_ge(attr_ready, 2 * i + j - 1)
                    sp.dma_start(AT_RAW[:, j, :], edge_attr_t[bass.ds(2 * i + j, 1), :, :]
                                 .rearrange("o p e -> (o p) e")).then_inc(attr_in[j], 16)
            for nt in range(NT):
                n = min(P, NODES - nt * P)
                sp.wait_ge(out_ready, nt + 1)
                sp.dma_start(out[nt * P:nt * P + n, :], H[0:n, nt, :]).then_inc(out_stored, 16)
            sp.wait_ge(out_stored, 16 * NT)

        @block.gpsimd
        def _(pool):
            nc.gpsimd.memset(IDENT[:, :], 0.0).then_inc(pool_const, 1)
            nc.gpsimd.iota(IOTA[:, :], [[1, NP]], base=0, channel_multiplier=0,
                           allow_small_or_imprecise_dtypes=True).then_inc(pool_const, 1)
            pool.wait_ge(pool_const, 2)
            nc.gpsimd.affine_select(out=IDENT[:, :], in_=IDENT[:, :], compare_op=ALU.not_equal, fill=1.0,
                                    base=0, pattern=[[-1, P]], channel_multiplier=1).then_inc(pool_const, 1)
            pool.wait_ge(idx_in, 32)
            held = [pool.alloc_register(f"pool_held{n}") for n in range(2)]

            def reached(n, value):
                if isinstance(value, int):
                    return value
                pool.reg_mov(held[n], value)
                return pool.snap(held[n])

            pool.wait_ge(h_stored, H_STORED)

            def gather0(i, first):
                for g in range(RING):
                    n = RING * i + g
                    summed, copied = reached(0, SUMS0 + GROUP * (n - RING + 1)), reached(1, n + 1)
                    pool.wait_ge(idx_in, 32)
                    if not first:
                        pool.wait_ge(agg_done, summed)
                    nc.gpsimd.tensor_copy(IDX[:, g, :], SRC[:, bass.ds(GROUP * n, GROUP)]).then_inc(idx_copied, 1)
                    pool.wait_ge(h_stored, H_STORED)
                    pool.wait_ge(idx_copied, copied)
                    for j in range(GROUP):
                        nc.gpsimd.indirect_dma_start(
                            ROWS0[:, g, j, :], None, h_tab[:, :],
                            bass.IndirectOffsetOnAxis(ap=IDX[:, g, j:j + 1], axis=0)).then_inc(gat0[g], 16)

            gather0(0, True)
            with pool.Fori(1, GROUPS // RING) as i:
                gather0(i, False)

            pool.wait_ge(pq_stored, PQ_STORED)
            pool.wait_ge(agg_done, SUMS0 + TILES)

            def gather_p(i, j):
                s = SLOTS * i + j
                in_psum, copied = reached(0, s - SLOTS + 1), reached(1, GROUPS + 2 * (s + 1))
                pool.wait_ge(idx_in, 32)
                if not isinstance(s, int) or s >= SLOTS:
                    pool.wait_ge(z1_done[1], in_psum)
                nc.gpsimd.tensor_copy(IDX[:, j, 0:2], SRC[:, bass.ds(2 * s, 2)]).then_inc(idx_copied, 1)
                nc.gpsimd.tensor_copy(IDX[:, j, 2:4], DST[:, bass.ds(2 * s, 2)]).then_inc(idx_copied, 1)
                pool.wait_ge(pq_stored, PQ_STORED)
                pool.wait_ge(idx_copied, copied)
                for k in range(2):
                    nc.gpsimd.indirect_dma_start(
                        GP[:, 2 * j + k, :], None, p_tab[:, :],
                        bass.IndirectOffsetOnAxis(ap=IDX[:, j, k:k + 1], axis=0)).then_inc(gat1[j], 16)

            def gather_q(i, j):
                p_rows = reached(0, 64 * i + 32)
                pool.wait_ge(pq_stored, PQ_STORED)
                pool.wait_ge(gat1[j], p_rows)
                for k in range(2):
                    nc.gpsimd.indirect_dma_start(
                        GP[:, 2 * j + k, :], None, q_tab[:, :],
                        bass.IndirectOffsetOnAxis(ap=IDX[:, j, 2 + k:3 + k], axis=0),
                        compute_op=ALU.add).then_inc(gat1[j], 16)

            gather_p(0, 0)
            for j in range(1, SLOTS):
                gather_p(0, j)
                gather_q(0, j - 1)
            with pool.Fori(1, PAIRS // SLOTS) as i:
                for j in range(SLOTS):
                    gather_p(i, j)
                    gather_q(i - (j == 0), (j - 1) % SLOTS)
            gather_q(PAIRS // SLOTS - 1, SLOTS - 1)

        @block.tensor
        def _(pe):
            extras = pe.alloc_register("pe_extras")
            pe.reg_mov(extras, 1)
            more = [pe.alloc_register(f"pe_more{n}") for n in range(2)]

            def load_extra(n, s):
                pe.load(more[n], pair_range(s, R_EXTRA, 1))
                return pe.snap(more[n])

            firsts, which = pe.alloc_register("pe_first"), pe.alloc_register("pe_which")

            def extra_tiles(s, more_tiles, bank, rows, added):
                with pe.If(more_tiles > 0):
                    pe.load(firsts, pair_range(s, R_FIRST, 1))
                    first = pe.snap(firsts, min_val=0, max_val=NT)
                    with pe.Fori(0, more_tiles) as k:
                        pe.reg_mov(which, (k - first + (1 << SIGN_BIT)) >> SIGN_BIT)
                        j = pe.snap(which, min_val=0, max_val=1)
                        n = pe.snap(extras)
                        pe.wait_ge(agg_done, added)
                        pe.wait_ge(xagg_done, n)
                        pe.wait_ge(xhot_ready, n + 1)
                        pe.matmul(bank, XHOT[:, :], rows(j), start=True, stop=True).then_inc(xseg_done, 1)
                        pe.reg_add(extras, extras, 1)

            pe.wait_ge(range_in, 16)

            def segment0(i, g):
                n = RING * i + g
                pe.wait_ge(gat0[g], 16 * GROUP * (i + 1))
                pe.wait_ge(hot_ready, GROUP * (n + 1))
                for j in range(GROUP):
                    pe.matmul(BANKS[:, GROUP * (g % 2) + j, :], HOT0[:, g, j, :], ROWS0[:, g, j, :],
                              start=True, stop=True).then_inc(seg_done, 1)

            def groups0(i, last):
                for g in range(RING):
                    n = RING * i + g
                    more_tiles = [load_extra(k, 2 * n + k) for k in range(2)]
                    if not last or g < RING - 1:
                        segment0(i + (g + 1) // RING, (g + 1) % RING)
                    with pe.If(more_tiles[0] + more_tiles[1] > 0):
                        for k in range(2):
                            extra_tiles(2 * n + k, more_tiles[k], BANKS[:, GROUP * (g % 2), :],
                                        lambda j: ROWS0[:, g, bass.ds(j + 2 * k, 1), :].rearrange("p o d -> p (o d)"),
                                        SUMS0 + GROUP * n + 1)

            segment0(0, 0)
            with pe.Fori(0, GROUPS // RING - 1) as i:
                groups0(i, False)
            groups0(GROUPS // RING - 1, True)

            freed = []

            def transposes(source, ready, count, moved, base, back=False):
                for nt in range(NT):
                    n = len(freed)
                    pe.wait_ge(ready, count(nt))
                    if n >= 2:
                        pe.wait_ge(*freed[n - 2])
                    for c in range(KD):
                        view = source[:, c, nt * P:(nt + 1) * P] if back else source[:, nt, c * P:(c + 1) * P]
                        mm = pe.transpose(SEG[:, n % 2, c * P:(c + 1) * P], view, IDENT[:, :])
                    mm.then_inc(tr_done, 1)
                    freed.append((moved, base + nt + 1))

            def product_t(base, weights, acts, kn, on, ready, count):
                with pe.Fori(0, BLOCKS) as b:
                    pe.wait_ge(ready, count(b))
                    for o in range(on):
                        pe.wait_ge(mm_moved, base + on * b + o + 1)
                        for k in range(kn):
                            mm = pe.matmul(Z2[:, o % 4, 0:BW], weights(k, o), acts(k, b), start=(k == 0), stop=(k == kn - 1))
                        mm.then_inc(mm_done, 1)

            pe.wait_ge(pool_const, 3)
            transposes(AGG, z0_ready, lambda nt: nt + 1, tr_moved, 0)
            pe.wait_ge(w01_in, 16 * KD)
            product_t(MM_1, lambda k, o: WA0[:, k, o * P:(o + 1) * P], lambda k, b: T1[:, k, bass.ds(b * BW, BW)], KD, KH,
                      tr_moved, lambda b: NT)
            pe.wait_ge(w02_in, 16 * KD)
            product_t(MM_2, lambda k, o: WB[:, k, o * P:(o + 1) * P], lambda k, b: H1T[:, k, bass.ds(b * BW, BW)], KH, KD,
                      bn_applied, lambda b: KH * (b + 1))
            transposes(T1, bn_applied, lambda nt: KH * BLOCKS + KD * (((nt + 1) * P - 1) // BW + 1),
                       r2_moved, 0, back=True)
            transposes(H, h_ready, lambda nt: NT + nt + 1, tr_moved, MOVED_H2)

            pe.wait_ge(w1_in, 16)
            for nt in range(NT):
                pe.wait_ge(tr_moved, MOVED_H2 + nt + 1)
                for part, moved, base in ((0, mm_moved, FREE + MM_PQ), (1, q_moved, 0)):
                    if nt >= 2:
                        pe.wait_ge(moved, base + nt - 1)
                    for k in range(KD):
                        mm = pe.matmul(Z2[:, 2 * part + nt % 2, :], T1[:, k, nt * P:(nt + 1) * P],
                                       WA[:, KD * part + k, :], start=(k == 0), stop=(k == KD - 1))
                    mm.then_inc(mm_done, 1)
            pe.wait_ge(mm_moved, FREE + MM_PQ + NT)
            pe.wait_ge(q_moved, NT)

            def z1(i, j):
                s = SLOTS * i + j
                pe.wait_ge(gat1[j], 64 * (i + 1))
                for b in range(2):
                    if not (isinstance(s, int) and s == 0):
                        pe.wait_ge(h_full[b], s)
                    for c in (2 * b, 2 * b + 1):
                        for k in range(2):
                            pe.matmul(Z1v[:, c, k * P:(k + 1) * P], GP[:, 2 * j + k, c * P:(c + 1) * P],
                                      IDENT[:, :], is_transpose=True, skip_group_check=True,
                                      start=(c == 2 * b and k == 0), stop=False)
                    pe.wait_ge(attr_ready, s + 1)
                    for c in (2 * b, 2 * b + 1):
                        for w in (WE_HI, WE_LO):
                            mm = pe.matmul(Z1v[:, c, :], w[:, c * P:(c + 1) * P], AT_R[:, j % 2, :],
                                           skip_group_check=True, start=False, stop=(w is WE_LO and c == 2 * b + 1))
                    mm.then_inc(z1_done[b], 1)

            def z2(s, j, k):
                if k == 0:
                    if not isinstance(s, int) or s >= 2:
                        pe.wait_ge(msg_ready, 1 + s - 1)
                    pe.wait_ge(h_lo[0], s + 1)
                    pe.wait_ge(h_lo[1], s + 1)
                at = Z2[:, 2 * j + k, :]
                pe.matmul(at, ONES_R[:, :], B2_R[:, :], start=True, stop=False)
                for c in range(KD):
                    e = slice(k * P, (k + 1) * P)
                    pe.matmul(at, H_LO[:, j, c, e], W2_HI[:, c, :], start=False, stop=False)
                    pe.matmul(at, H_HI[:, j, c, e], W2_LO[:, c, :], start=False, stop=False)
                    mm = pe.matmul(at, H_HI[:, j, c, e], W2_HI[:, c, :], start=False, stop=(c == KD - 1))
                if k == 1:
                    mm.then_inc(z2_done, 1)

            def segment1(s):
                pe.wait_ge(msg_ready, 1 + s + 1)
                for j in range(2):
                    pe.matmul(SEG[:, j, :], ONEHOT[:, j, :], MSG[:, j, :], start=True, stop=True).then_inc(seg_done, 1)

            def extras1(s, more_tiles):
                extra_tiles(s, more_tiles, SEG[:, 0, :],
                            lambda j: MSG[:, bass.ds(j, 1), :].rearrange("p o d -> p (o d)"), SUMS1 + 2 * s + 1)

            def edge_step(i, j, first):
                s = SLOTS * i + j
                if not first:
                    more_tiles = load_extra(0, s - 3)
                z1(i, j)
                if not first:
                    extras1(s - 3, more_tiles)
                for k in range(2):
                    z2(s - 1, (j - 1) % 2, k)
                segment1(s - 2)

            z1(0, 0)
            z1(0, 1)
            for k in range(2):
                z2(0, 0, k)
            for j in range(2, SLOTS):
                edge_step(0, j, j == 2)
            with pe.Fori(1, PAIRS // SLOTS) as i:
                for j in range(SLOTS):
                    edge_step(i, j, False)
            more_tiles = load_extra(0, PAIRS - 3)
            extras1(PAIRS - 3, more_tiles)
            for k in range(2):
                z2(PAIRS - 1, 1, k)
            for s in (PAIRS - 2, PAIRS - 1):
                segment1(s)
                extras1(s, load_extra(0, s))

            transposes(AGG, agg_done, lambda nt: SUMS1 + TILES, tr_moved, MOVED_AGG)
            transposes(H, h_ready, lambda nt: 2 * NT, tr_moved, MOVED_H3)
            pe.wait_ge(w3_in, 16)
            pe.wait_ge(tr_moved, MOVED_H3 + NT)
            with pe.Fori(0, BLOCKS) as b:
                for o in range(KD):
                    pe.wait_ge(u_ready, KD * b + o + 1)
                    for k in range(2 * KD):
                        a = (T1 if k < KD else AT2)[:, k % KD, bass.ds(b * BW, BW)]
                        mm = pe.matmul(Z2[:, o, 0:BW], WB[:, k, o * P:(o + 1) * P], a, start=(k == 0), stop=(k == 2 * KD - 1))
                    mm.then_inc(mm_done, 1)
            pe.wait_ge(w4_in, 16)
            for nt in range(NT):
                pe.wait_ge(u_ready, KD + KD * (((nt + 1) * P - 1) // BW + 1))
                if nt >= 2:
                    pe.wait_ge(y_moved, nt - 1)
                for k in range(KD):
                    mm = pe.matmul(SEG[:, nt % 2, :], UT[:, k, nt * P:(nt + 1) * P], W4[:, k, :],
                                   start=(k == 0), stop=(k == KD - 1))
                mm.then_inc(y_done, 1)

        @block.scalar
        def _(act):
            def std(n, var, count):
                act.wait_ge(var_ready, count)
                nc.scalar.activation(TMP[:, 3, 0:n], var, ACT.Sqrt, bias=CONST[:, 1:2]).then_inc(std_ready, 1)

            def normalise(target, source, func, base, done, between=lambda g: None):
                for g, (a, b) in enumerate(LN_GROUPS):
                    act.wait_ge(var_ready, base + g + 1)
                    nc.scalar.activation(TMP[:, 4, a:b], LN_MV[:, a:b, 1], ACT.Sqrt, bias=CONST[:, 1:2]).then_inc(std_ready, 1)
                    act.wait_ge(scale_ready, ln_groups[0] + 1)
                    ln_groups[0] += 1
                    for nt in range(a, b):
                        nc.scalar.activation(target[:, nt, :], source[:, nt, :], func, bias=NBIAS[:, nt:nt + 1],
                                             scale=RSTD[:, nt:nt + 1]).then_inc(done, 1)
                    between(g)

            ln_groups = [0]
            moves = [0]

            def move_t(target, scale=1.0, tiles=range(NT)):
                for nt in tiles:
                    n = moves[0]
                    act.wait_ge(tr_done, n + 1)
                    nc.scalar.mul(target[:, :, nt * P:(nt + 1) * P],
                                  SEG[:, n % 2, :].rearrange("p (c e) -> p c e", c=KD), scale).then_inc(tr_moved, 1)
                    moves[0] += 1

            def move_product(base, target, on, bias):
                with act.Fori(0, BLOCKS) as b:
                    for o in range(on):
                        act.wait_ge(mm_done, base + on * b + o + 1)
                        nc.scalar.activation(target[:, o, bass.ds(b * BW, BW)], Z2[:, o % 4, 0:BW], ACT.Identity,
                                             bias=COLS[:, bias + o:bias + o + 1]).then_inc(mm_moved, 1)

            def apply_bn(target, on, count):
                act.wait_ge(bn_ready, count)
                for b in range(BLOCKS):
                    for o in range(on):
                        at = target[:, o, b * BW:(b + 1) * BW]
                        nc.scalar.activation(at, at, ACT.Relu, bias=SHIFT[:, o:o + 1], scale=SCALE[:, o:o + 1]).then_inc(bn_applied, 1)

            act.wait_ge(dve_const, 1)
            normalise(H, X, ACT.Relu, 0, h_ready)
            act.wait_ge(small_in, 32)
            move_t(T1)
            move_product(MM_1, H1T, KH, CB1)
            std(KH, MV[:, 0:KH, 1], LG + 1)
            apply_bn(H1T, KH, 1)
            move_product(MM_2, T1, KD, CB2)
            std(KD, MV[:, 0:KD, 1], LG + 2)
            apply_bn(T1, KD, 2)
            moves[0] += NT
            act.wait_ge(h_stored, H_STORED)
            def move_group(g):
                if g >= 0:
                    move_t(T1, tiles=range(*LN_GROUPS[g]))
            normalise(H, X, ACT.Relu, LG + 2, h_ready, lambda g: move_group(g - 1))
            move_group(LG - 1)
            for nt in range(NT):
                act.wait_ge(mm_done, MM_PQ + 2 * nt + 1)
                nc.scalar.copy(AGG[:, nt, :], Z2[:, nt % 2, :]).then_inc(mm_moved, 1)

            nc.scalar.preload_act_table_set("natural_log_exp_and_others")

            def exp1(s, h):
                act.wait_ge(z1_done[h], s + 1)
                if not (isinstance(s, int) and s == 0):
                    act.wait_ge(h_full[h], s)
                nc.scalar.activation(EA[:, 2 * h:2 * h + 2, :], Z1v[:, 2 * h:2 * h + 2, :], ACT.Exp).then_inc(a_exp[h], 1)

            def log1(s, h):
                act.wait_ge(a_sq[h], s + 1)
                nc.scalar.activation(EA[:, 2 * h:2 * h + 2, :], EA[:, 2 * h:2 * h + 2, :], ACT.Ln, bias=CONST[:, 0:1]).then_inc(a_ln[h], 1)

            def inv1(s, h):
                act.wait_ge(a_ln[h], s + 1)
                nc.scalar.activation(EA[:, 2 * h:2 * h + 2, :], EA[:, 2 * h:2 * h + 2, :], ACT.Exp, scale=-1.0).then_inc(a_r[h], 1)

            def hi1(s, j, h):
                act.wait_ge(h_full[h], s + 1)
                if not isinstance(s, int) or s >= 2:
                    act.wait_ge(z2_done, s - 1)
                nc.scalar.copy(H_HI[:, j, 2 * h:2 * h + 2, :], HF[:, 2 * h:2 * h + 2, :]).then_inc(h_hi[h], 1)

            def exp2(s, j):
                act.wait_ge(z2_done, s + 1)
                act.wait_ge(msg_ready, 1 + s)
                nc.scalar.activation(EB[:, :, :], Z2[:, 2 * j:2 * j + 2, :], ACT.Exp).then_inc(b_exp, 1)

            def sq2(s):
                act.wait_ge(b_cut, s + 1)
                nc.scalar.activation(EB[:, :, :], EB[:, :, :], ACT.Square).then_inc(b_sq, 1)

            def log2(s):
                act.wait_ge(b_sq, s + 1)
                nc.scalar.activation(EB[:, :, :], EB[:, :, :], ACT.Ln, bias=CONST[:, 0:1]).then_inc(b_ln, 1)

            def inv2(s):
                act.wait_ge(b_ln, s + 1)
                nc.scalar.activation(EB[:, :, :], EB[:, :, :], ACT.Exp, scale=-1.0).then_inc(b_r, 1)

            def attr_high(i, j):
                s = 2 * i + j
                act.wait_ge(attr_in[j], 16 * (i + 1))
                if not isinstance(s, int) or s >= 2:
                    act.wait_ge(z1_done[1], s - 1)
                nc.scalar.copy(AT_R[:, j, :], AT_RAW[:, j, :]).then_inc(attr_hi, 1)

            def mish_a(s, j):
                for h in range(2):
                    exp1(s, h)
                for h in range(2):
                    log1(s, h)
                for h in range(2):
                    inv1(s, h)
                for h in range(2):
                    hi1(s, j, h)

            def mish_b(s, j):
                exp2(s, j)
                sq2(s)
                log2(s)
                inv2(s)

            def edge_step(i, j, more):
                s = 2 * i + j
                exp2(s - 2, j)
                exp1(s, 0)
                sq2(s - 2)
                exp1(s, 1)
                log2(s - 2)
                inv2(s - 2)
                for step in (log1, inv1):
                    for h in range(2):
                        step(s, h)
                if more:
                    attr_high(i + j, 1 - j)
                for h in range(2):
                    hi1(s, j, h)

            for j in range(2):
                attr_high(0, j)
            mish_a(0, 0)
            attr_high(1, 0)
            mish_a(1, 1)
            with act.Fori(1, PAIRS // 2 - 1) as i:
                for j in range(2):
                    edge_step(i, j, True)
            for j in range(2):
                edge_step(PAIRS // 2 - 1, j, j == 0)
            mish_b(PAIRS - 2, 0)
            mish_b(PAIRS - 1, 1)

            move_t(AT2, scale=-2.0)
            move_t(T1)
            with act.Fori(0, BLOCKS) as b:
                for o in range(KD):
                    n = KD * b + o
                    act.wait_ge(mm_done, MM_PQ + 2 * NT + n + 1)
                    nc.scalar.activation(UT[:, o, bass.ds(b * BW, BW)], Z2[:, o, 0:BW], ACT.Identity,
                                         bias=COLS[:, CB3 + o:CB3 + o + 1]).then_inc(u_bias, 1)
                    act.wait_ge(u_cut, n + 1)
                    nc.scalar.activation(XWORK, XWORK, ACT.Exp).then_inc(u_exp, 1)
                    act.wait_ge(u_exp, n + 1)
                    nc.scalar.activation(XWORK, XWORK, ACT.Square, bias=CONST[:, 0:1]).then_inc(u_sq, 1)
                    act.wait_ge(u_sq, n + 1)
                    nc.scalar.activation(XWORK, XWORK, ACT.Ln, bias=CONST[:, 0:1]).then_inc(u_ln, 1)
                    act.wait_ge(u_ln, n + 1)
                    nc.scalar.activation(XWORK, XWORK, ACT.Exp, scale=-1.0).then_inc(u_r, 1)
            normalise(AGG, AGG, ACT.Identity, 2 * LG + 2, norm_done)

        @block.vector
        def _(dve):
            chain = [0]

            def link(ins):
                chain[0] += 1
                ins.then_inc(dve_chain, 1)
                dve.wait_ge(dve_chain, chain[0])

            extras = dve.alloc_register("dve_extras")
            dve.reg_mov(extras, 1)

            def ln_stats(source, g):
                a, b = LN_GROUPS[g]
                for nt in range(a, b):
                    nc.vector.bn_stats(STATS[:, nt, :], source[:, nt, :]).then_inc(dve_chain, 1)
                chain[0] += b - a
                for nt in range(a, b):
                    dve.wait_ge(dve_chain, chain[0] - (b - 1 - nt))
                    ins = nc.vector.bn_aggr(LN_MV[:, nt, :], STATS[:, nt, :])
                    if nt == b - 1:
                        ins.then_inc(var_ready, 1)

            def ln_scale(g, count):
                a, b = LN_GROUPS[g]
                dve.wait_ge(std_ready, count + g + 1)
                link(nc.vector.reciprocal(RSTD[:, a:b], TMP[:, 4, a:b]))
                nc.vector.scalar_tensor_tensor(NBIAS[:, a:b], LN_MV[:, a:b, 0], -1.0, RSTD[:, a:b],
                                               ALU.mult, ALU.mult).then_inc(scale_ready, 1)

            def batch_norm(source, on, gamma, beta, base, count):
                for b, (first, end) in enumerate(BN_PIECES):
                    for o in range(on):
                        dve.wait_ge(mm_moved, FREE + base + on * b + o + 1)
                        nc.vector.bn_stats(BSTATS[:, o, 6 * b:6 * b + 6], source[:, o, first:end]).then_inc(dve_chain, 1)
                        chain[0] += 1
                dve.wait_ge(dve_chain, chain[0])
                for o in range(on):
                    ins = nc.vector.bn_aggr(MV[:, o, :], BSTATS[:, o, :])
                    ins.then_inc(dve_chain, 1) if o < on - 1 else ins.then_inc(var_ready, 1)
                    chain[0] += o < on - 1
                dve.wait_ge(dve_chain, chain[0])
                dve.wait_ge(var_ready, count)
                dve.wait_ge(std_ready, count)
                link(nc.vector.reciprocal(TMP[:, 0, 0:on], TMP[:, 3, 0:on]))
                link(nc.vector.tensor_tensor(SCALE[:, 0:on], TMP[:, 0, 0:on], COLS[:, gamma:gamma + on], ALU.mult))
                link(nc.vector.tensor_tensor(TMP[:, 1, 0:on], MV[:, 0:on, 0], SCALE[:, 0:on], ALU.mult))
                nc.vector.tensor_tensor(SHIFT[:, 0:on], COLS[:, beta:beta + on], TMP[:, 1, 0:on], ALU.subtract).then_inc(bn_ready, 1)

            low_regs = [[dve.alloc_register(f"dve_low{n}_{j}") for j in range(R_USED)] for n in range(2 * RING)]

            which, past_low = dve.alloc_register("dve_which"), dve.alloc_register("dve_past_low")

            def load_range(n, s):
                dve.load(low_regs[n], pair_range(s, R_LOW, R_USED))

            def low_tile(n, j):
                return dve.snap(low_regs[n][j], min_val=0, max_val=NT - 1)

            def hot(at, tile, low):
                nc.vector.tensor_scalar(at, IOTA[:, bass.ds(low * P, P)], DSTF[:, bass.ds(tile, 1)], None,
                                        ALU.is_equal).then_inc(hot_ready, 1)

            def add_sums(low, bank):
                a = AGG[:, bass.ds(low, 1), :].rearrange("p o d -> p (o d)")
                nc.vector.tensor_tensor(a, a, bank, ALU.add).then_inc(agg_done, 1)

            def sums_extra(s, n, bank, added):
                more_tiles = dve.snap(low_regs[n][R_EXTRA], min_val=0, max_val=2 * NT)
                with dve.If(more_tiles > 0):
                    first = dve.snap(low_regs[n][R_FIRST], min_val=0, max_val=NT)
                    low = dve.snap(low_tile(n, 0) + 1)
                    step = dve.snap(low_tile(n, 1) - low_tile(n, 0) - first)
                    with dve.Fori(0, more_tiles) as k:
                        dve.reg_mov(which, (k - first + (1 << SIGN_BIT)) >> SIGN_BIT)
                        j = dve.snap(which, min_val=0, max_val=1)
                        dve.reg_mov(past_low, low + k + j * step)
                        nt = dve.snap(past_low, min_val=0, max_val=NT - 1)
                        n_extra = dve.snap(extras)
                        dve.wait_ge(agg_done, added)
                        dve.wait_ge(xseg_done, n_extra)
                        dve.wait_ge(xagg_done, n_extra)
                        nc.vector.tensor_scalar(XHOT[:, :], IOTA[:, bass.ds(nt * P, P)], DSTF[:, bass.ds(2 * s + j, 1)],
                                                None, ALU.is_equal).then_inc(xhot_ready, 1)
                        dve.wait_ge(xseg_done, n_extra + 1)
                        a = AGG[:, bass.ds(nt, 1), :].rearrange("p o d -> p (o d)")
                        nc.vector.tensor_tensor(a, a, bank, ALU.add).then_inc(xagg_done, 1)
                        dve.reg_add(extras, extras, 1)

            def wait_extras():
                extra = dve.snap(extras)
                dve.wait_ge(xagg_done, extra)

            nc.vector.memset(CONST[:, 0:1], 1.0).then_inc(dve_chain, 1)
            nc.vector.memset(B2_R[:, :].bitcast(F32), 0.0).then_inc(dve_chain, 1)
            nc.vector.memset(ONES_R[:, :].bitcast(F32), 1.0).then_inc(dve_chain, 1)
            chain[0] += 3
            for n, (start, count) in enumerate(((mm_moved, FREE), (u_ready, KD), (msg_ready, 1),
                                                (xhot_ready, 1), (xseg_done, 1), (xagg_done, 1))):
                nc.vector.memset(TMP[:, 0, n:n + 1], 0.0).then_inc(start, count)
            nc.vector.memset(CONST[:, 1:2], LN_EPS).then_inc(dve_const, 1)
            link(nc.vector.memset(RNG_T[:, :], 0))
            dve.wait_ge(drow_in, 16)
            low, high, past = RNG_T[:, R_LOW:R_LOW + 2], RNG_T[:, R_WORK:R_WORK + 2], RNG_T[:, R_WORK + 2:R_WORK + 4]
            nc.vector.tensor_reduce(low, DROW[:, :, :], AX.X, ALU.min).then_inc(dve_chain, 1)
            nc.vector.tensor_reduce(high, DROW[:, :, :], AX.X, ALU.max).then_inc(dve_chain, 1)
            chain[0] += 2
            dve.wait_ge(dve_chain, chain[0])
            link(nc.vector.tensor_scalar(RNG_T[:, :], RNG_T[:, :], P.bit_length() - 1, None, ALU.arith_shift_right))
            link(nc.vector.tensor_tensor(past, high, low, ALU.subtract))
            nc.vector.tensor_copy(RNG_T[:, R_FIRST:R_FIRST + 1], past[:, 0:1]).then_inc(range_ready, 1)
            nc.vector.tensor_tensor(RNG_T[:, R_EXTRA:R_EXTRA + 1], past[:, 0:1], past[:, 1:2], ALU.add).then_inc(range_ready, 1)
            for g in range(LG):
                dve.wait_ge(x_in[g], 16)
                ln_stats(X, g)
                if g > 0:
                    ln_scale(g - 1, 0)
            ln_scale(LG - 1, 0)
            dve.wait_ge(idx_in, 32)
            link(nc.vector.tensor_copy(DSTF[:, :], DST[:, :]))
            nc.vector.memset(AGG[:, :, :], 0.0).then_inc(agg_done, 1)
            dve.wait_ge(small_in, 32)
            link(nc.vector.tensor_scalar(EPS1[:, :], EPS1[:, :], 1.0, None, ALU.add))

            dve.wait_ge(pool_const, 3)
            dve.wait_ge(range_in, 16)

            def load0(n, g):
                for k in range(2):
                    load_range(2 * g + k, 2 * n + k)

            def low0(g, j):
                return low_tile(2 * g + j // 2, j % 2)

            def hot0(n, g, j):
                hot(HOT0[:, g, j, :], GROUP * n + j, low0(g, j))

            def add0(n, g, j):
                dve.wait_ge(agg_done, SUMS0 + GROUP * n + j)
                add_sums(low0(g, j), BANKS[:, GROUP * (g % 2) + j, :])

            def group0(n, g, ahead):
                g2 = (g + 2) % RING
                dve.wait_ge(seg_done, GROUP * (n + 1))
                add0(n, g, 0)
                if ahead:
                    load0(n + 2, g2)
                add0(n, g, 1)
                if ahead:
                    hot0(n + 2, g2, 0)
                add0(n, g, 2)
                if ahead:
                    hot0(n + 2, g2, 1)
                past = [dve.snap(low_regs[2 * g + k][R_EXTRA]) for k in range(2)]
                with dve.If(past[0] + past[1] > 0):
                    for k in range(2):
                        sums_extra(2 * n + k, 2 * g + k, BANKS[:, GROUP * (g % 2), :], SUMS0 + GROUP * (n + 1) - 1)
                wait_extras()
                add0(n, g, 3)
                if ahead:
                    hot0(n + 2, g2, 2)
                    hot0(n + 2, g2, 3)

            for g in range(2):
                load0(g, g)
                for j in range(GROUP):
                    hot0(g, g, j)
            with dve.Fori(0, GROUPS // RING - 1) as i:
                for g in range(RING):
                    group0(RING * i + g, g, True)
            for g in range(RING):
                group0(GROUPS - RING + g, g, g < RING - 2)
            dve.wait_ge(agg_done, SUMS0 + TILES)
            dve.wait_ge(h_ready, NT)
            for nt in range(NT):
                nc.vector.scalar_tensor_tensor(AGG[:, nt, :], H[:, nt, :], EPS1[:, 0:1], AGG[:, nt, :],
                                               ALU.mult, ALU.add).then_inc(z0_ready, 1)
            link(nc.vector.tensor_tensor(X[:, :, :], X[:, :, :], H[:, :, :], ALU.add))
            batch_norm(H1T, KH, CG1, CBE1, MM_1, LG + 1)
            dve.wait_ge(split_in, 48)
            dve.wait_ge(rows_in, 16)
            link(nc.vector.tensor_scalar(W2_RAW, W2_RAW, -2.0, None, ALU.mult))
            nc.vector.tensor_copy(W2_HI[:, :, :], W2_RAW).then_inc(dve_chain, 1)
            nc.vector.tensor_copy(WE_HI[:, :], WE_RAW).then_inc(dve_chain, 1)
            nc.vector.tensor_copy(B2_R[0:1, :], ROWS[0:1, ROW_B2, :]).then_inc(dve_chain, 1)
            nc.vector.tensor_copy(B2_R[32:33, :], ROWS[32:33, ROW_B2, :]).then_inc(dve_chain, 1)
            chain[0] += 4
            dve.wait_ge(dve_chain, chain[0])
            nc.vector.tensor_tensor(W2_LO[:, :, :], W2_RAW, W2_HI[:, :, :].bitcast(F32), ALU.subtract).then_inc(dve_chain, 1)
            nc.vector.tensor_tensor(WE_LO[:, :], WE_RAW, WE_HI[:, :].bitcast(F32), ALU.subtract).then_inc(dve_chain, 1)
            nc.vector.tensor_tensor(B2_R[32:33, :], ROWS[32:33, ROW_B2, :], B2_R[32:33, :].bitcast(F32), ALU.subtract).then_inc(dve_chain, 1)
            chain[0] += 3
            dve.wait_ge(dve_chain, chain[0])
            batch_norm(T1, KD, CG2, CBE2, MM_2, LG + 2)
            for g, (a, b) in enumerate(LN_GROUPS):
                for nt in range(a, b):
                    dve.wait_ge(tr_done, TR_R2 + nt + 1)
                    nc.vector.tensor_tensor(X[:, nt, :], X[:, nt, :], SEG[:, (TR_R2 + nt) % 2, :], ALU.add).then_inc(r2_moved, 1)
                dve.wait_ge(r2_moved, b)
                ln_stats(X, g)
                if g > 0:
                    ln_scale(g - 1, LG + 2)
            ln_scale(LG - 1, LG + 2)
            for nt in range(NT):
                dve.wait_ge(mm_done, MM_PQ + 2 * nt + 2)
                nc.vector.tensor_tensor(QST[:, nt, :], Z2[:, 2 + nt % 2, :], ROWS[:, ROW_B1, :], ALU.add).then_inc(q_moved, 1)
            dve.wait_ge(pq_stored, PQ_STORED)
            nc.vector.memset(AGG[:, :, :], 0.0).then_inc(agg_done, 1)

            def attr_rest(s, j):
                dve.wait_ge(attr_hi, s + 1)
                low = AT_R[EDGE_DIM:P, j, :]
                nc.vector.tensor_tensor(low, AT_RAW[EDGE_DIM:P, j, :], low.bitcast(F32), ALU.subtract).then_inc(attr_ready, 1)

            def cut1(s, h):
                dve.wait_ge(a_exp[h], s + 1)
                at = EA[:, 2 * h:2 * h + 2, :]
                nc.vector.tensor_scalar(at, at, E_MAX, 1.0, ALU.min, ALU.add).then_inc(a_cut[h], 1)

            def sq1(s, h):
                dve.wait_ge(a_cut[h], s + 1)
                at = EA[:, 2 * h:2 * h + 2, :]
                nc.vector.tensor_tensor(at, at, at, ALU.mult).then_inc(a_sq[h], 1)

            def full1(s, h):
                dve.wait_ge(a_r[h], s + 1)
                if not (isinstance(s, int) and s == 0):
                    dve.wait_ge(h_lo[h], s)
                nc.vector.scalar_tensor_tensor(HF[:, 2 * h:2 * h + 2, :].rearrange("p c e -> p (c e)"),
                                               EA[:, 2 * h:2 * h + 2, :].rearrange("p c e -> p (c e)"),
                                               -0.5, Z1[:, h, :], ALU.add, ALU.mult).then_inc(h_full[h], 1)

            def lo1(s, j, h):
                dve.wait_ge(h_hi[h], s + 1)
                c = slice(2 * h, 2 * h + 2)
                nc.vector.tensor_tensor(H_LO[:, j, c, :], HF[:, c, :], H_HI[:, j, c, :].bitcast(F32), ALU.subtract).then_inc(h_lo[h], 1)

            def cut2(s):
                dve.wait_ge(b_exp, s + 1)
                nc.vector.tensor_scalar(EB[:, :, :], EB[:, :, :], E_MAX, 1.0, ALU.min, ALU.add).then_inc(b_cut, 1)

            def hots1(s, n):
                for k in range(2):
                    hot(ONEHOT[:, k, :], 2 * s + k, low_tile(n, k))

            def message(s, j):
                dve.wait_ge(b_r, s + 1)
                nc.vector.scalar_tensor_tensor(MSG[:, :, :].rearrange("p k d -> p (k d)"), EB[:, :, :].rearrange("p k d -> p (k d)"),
                                               -0.5, Z2[:, 2 * j:2 * j + 2, :].rearrange("p k d -> p (k d)"),
                                               ALU.add, ALU.mult).then_inc(msg_ready, 1)

            def sums1(s, n):
                wait_extras()
                dve.wait_ge(seg_done, TILES + 2 * (s + 1))
                for j in range(2):
                    dve.wait_ge(agg_done, SUMS1 + 2 * s + j)
                    add_sums(low_tile(n, j), SEG[:, j, :])
                sums_extra(s, n, SEG[:, 0, :], SUMS1 + 2 * (s + 1))

            def mish_a(s, j):
                for step in (cut1, sq1, full1):
                    for h in range(2):
                        step(s, h)
                for h in range(2):
                    lo1(s, j, h)

            def mish_b(s, j):
                load_range(j, s)
                cut2(s)
                sums1(s - 1, 1 - j)
                hots1(s, j)
                message(s, j)

            def edge_step(s, j, first, more):
                load_range(j, s - 2)
                cut2(s - 2)
                if not first:
                    sums1(s - 3, 1 - j)
                hots1(s - 2, j)
                for h in range(2):
                    cut1(s, h)
                    sq1(s, h)
                message(s - 2, j)
                for h in range(2):
                    full1(s, h)
                if more:
                    attr_rest(s + 1, 1 - j)
                for h in range(2):
                    lo1(s, j, h)

            for j in range(2):
                attr_rest(j, j)
            mish_a(0, 0)
            attr_rest(2, 0)
            mish_a(1, 1)
            for j in range(2):
                edge_step(2 + j, j, j == 0, True)
            with dve.Fori(2, PAIRS // 2 - 1) as i:
                for j in range(2):
                    edge_step(2 * i + j, j, False, True)
            for j in range(2):
                edge_step(PAIRS - 2 + j, j, False, j == 0)
            mish_b(PAIRS - 2, 0)
            mish_b(PAIRS - 1, 1)
            sums1(PAIRS - 1, 1)
            dve.wait_ge(agg_done, SUMS1 + TILES)

            with dve.Fori(0, BLOCKS) as b:
                for o in range(KD):
                    n = KD * b + o
                    at = UT[:, o, bass.ds(b * BW, BW)]
                    dve.wait_ge(u_bias, n + 1)
                    dve.wait_ge(u_ready, KD + n)
                    nc.vector.tensor_scalar(XWORK, at, Z_MAX, None, ALU.min).then_inc(u_cut, 1)
                    dve.wait_ge(u_r, n + 1)
                    nc.vector.scalar_tensor_tensor(at, XWORK, -0.5, at, ALU.add, ALU.mult).then_inc(u_ready, 1)
            def wide(row):
                return ROWS[:, row:row + 1, :].broadcast_to([P, NT, DIM])
            dve.wait_ge(tr_moved, MOVED_H3 + NT)
            link(nc.vector.tensor_tensor(H[:, :, :], H[:, :, :], wide(ROW_B4), ALU.add))
            link(nc.vector.tensor_tensor(X[:, :, :], X[:, :, :], wide(ROW_BETA), ALU.add))
            def finish(g):
                a, b = LN_GROUPS[g]
                for nt in range(a, b):
                    dve.wait_ge(norm_done, nt + 1)
                    link(nc.vector.tensor_tensor(AGG[:, nt, :], AGG[:, nt, :], ROWS[:, ROW_GAMMA, :], ALU.mult))
                    nc.vector.tensor_tensor(H[:, nt, :], AGG[:, nt, :], X[:, nt, :], ALU.add).then_inc(out_ready, 1)

            for g, (a, b) in enumerate(LN_GROUPS):
                for nt in range(a, b):
                    dve.wait_ge(y_done, nt + 1)
                    nc.vector.scalar_tensor_tensor(AGG[:, nt, :], SEG[:, nt % 2, :], -2.0, H[:, nt, :], ALU.mult, ALU.add).then_inc(y_moved, 1)
                dve.wait_ge(y_moved, b)
                ln_stats(AGG, g)
                if g > 0:
                    ln_scale(g - 1, 2 * LG + 2)
                    finish(g - 1)
            ln_scale(LG - 1, 2 * LG + 2)
            finish(LG - 1)


def kernel(**inputs):
    import numpy as np
    import concourse.bacc as bacc
    from concourse.bass_utils import run_bass_kernel_spmd

    get = lambda name: np.asarray(inputs[name])
    x = np.zeros((NP, DIM), np.float32)
    x[:NODES] = get("x")
    src = np.zeros(TILES * P, np.int32)
    src[:EDGES] = get("src")
    dst = np.full(TILES * P, NP - 1, np.int32)
    dst[:EDGES] = get("dst")
    attr = np.zeros((TILES * P, EDGE_DIM), np.float32)
    attr[:EDGES] = get("edge_attr_64")
    attr = attr.reshape(PAIRS, PW, EDGE_DIM).transpose(0, 2, 1)
    columns = ["L0_gnn_b1", "L0_gnn_g1", "L0_gnn_be1", "L0_gnn_b2", "L0_gnn_g2", "L0_gnn_be2", "L1_gnn_b3"]
    rows = ["L1_gnn_b1", "L1_gnn_b2", "L1_gnn_b4", "L1_gnn_gamma", "L1_gnn_beta"]
    arrays = {
        "x": x,
        "src_cols": src.reshape(TILES, P).T,
        "dst_cols": dst.reshape(TILES, P).T,
        "dst_rows": dst.reshape(PAIRS, 2, P),
        "edge_attr_t": np.concatenate([attr, attr], axis=1),
        "eps": get("L0_gnn_eps").reshape(1),
        "cols": np.concatenate([get(n).reshape(-1, P).T for n in columns], axis=1),
        "rows": np.stack([get(n) for n in rows]),
        "w01": get("L0_gnn_W1"), "w02": get("L0_gnn_W2"),
        "w1": get("L1_gnn_W1"), "w2": get("L1_gnn_W2"), "w3": get("L1_gnn_W3"), "w4": get("L1_gnn_W4"),
    }
    nc = bacc.Bacc("TRN2", target_bir_lowering=False, num_devices=1)
    feeds, args = {}, {}
    for name, a in arrays.items():
        a = np.ascontiguousarray(a)
        feeds[f"in_{name}"] = a
        args[name] = nc.dram_tensor(f"in_{name}", a.shape, mybir.dt.from_np(a.dtype), kind="ExternalInput").ap()
    args["out"] = nc.dram_tensor("out_x", (NODES, DIM), F32, kind="ExternalOutput").ap()
    gnn_kernel(nc, **args)
    r = run_bass_kernel_spmd(nc, [feeds], core_ids=[0])
    return r.results[0]["out_x"]
```

```python
from contextlib import ExitStack

import concourse.bass as bass
from concourse import mybir

ALU = mybir.AluOpType
ACT = mybir.ActivationFunctionType
F32 = mybir.dt.float32
F32R = mybir.dt.float32r
I32 = mybir.dt.int32
AX = mybir.AxisListType

P = 128
NODES, DIM, HID0, EDGE_DIM = 1250, 512, 1024, 64
EDGES = 20000
NT = -(-NODES // P)
NP = NT * P
KD = DIM // P
KH = HID0 // P
GROUP = 4
RING = 4
TILES = -(-EDGES // (GROUP * RING * P)) * GROUP * RING
GROUPS = TILES // GROUP
PAIRS = TILES // 2
R_LOW, R_EXTRA, R_NEXT, R_WRAP, R_WORDS = range(5)
R_USED = 3
PW = 2 * P
EDGE_PAIRS = -(-EDGES // PW)
LAST = (EDGE_PAIRS - 1) // 2
SLOTS = 4
BLOCKS = 4
BW = NP // BLOCKS
LN_EPS = BN_EPS = 1e-5
E_MAX = 1e9
Z_MAX = 20.0
BN_PIECES = [(b * BW, min((b + 1) * BW, NODES)) for b in range(BLOCKS)]
LN_GROUPS = [(a, min(a + 3, NT)) for a in range(0, NT, 3)]
LG = len(LN_GROUPS)
CB1, CG1, CBE1, CB2, CG2, CBE2, CB3 = 0, 8, 16, 24, 28, 32, 36
NCOLS = 40
ROW_B1, ROW_B2, ROW_B4, ROW_GAMMA, ROW_BETA = range(5)


def gnn_kernel(nc, x, src_cols, dst_cols, dst_rows, edge_attr_t, eps, cols, rows, w01, w02,
               w1, w2, w3, w4, out):
    ctx = ExitStack()
    with ctx:
        place = [nc.sbuf_base + (-nc.sbuf_base) % 64]

        def sb(name, shape, dt=F32, at=None):
            size = 4
            for n in shape[1:]:
                size *= n
            if at is None:
                at = place[0]
                place[0] += size + (-size) % 32
            return nc.alloc_sbuf_tensor_at(name, shape, dt, offset=at), at + size + (-size) % 32

        X, _ = sb("x_nodes", [P, NT, DIM])
        h_at = place[0]
        H, agg_at = sb("h_nodes", [P, NT, DIM])
        AGG, _ = sb("agg_nodes", [P, NT, DIM])
        t1_at = place[0]
        T1, _ = sb("act_t", [P, KD, NP])
        h1t_at = place[0]
        H1T, _ = sb("hidden_t", [P, KH, NP])
        wa_at = place[0]
        WA, wb_at = sb("weights_a", [P, 2 * KD, DIM])
        WB, w2_at = sb("weights_b", [P, 2 * KD, DIM])
        WA0 = WA[:, :, :].rearrange("p (k h) n -> p k (h n)", k=KD)
        UPAIRS = KD // 2
        W2_HI, _ = sb("w2_hi", [P, KD, DIM], F32R)
        W2_LO, _ = sb("w2_lo", [P, KD, DIM], F32R)
        WE_HI, _ = sb("we_hi", [P, DIM], F32R)
        WE_LO, w2_end = sb("we_lo", [P, DIM], F32R)
        b2_at = place[0]
        B2_R, _ = sb("b2_parts", [64, DIM], F32R)
        ONES_R, _ = sb("ones", [64, P], F32R)
        ROWS, _ = sb("rows", [P, 5, DIM])
        IDENT, _ = sb("ident", [P, P])
        SRC, _ = sb("src", [P, TILES], I32)
        DST, _ = sb("dst", [P, TILES], I32)
        REL_G, _ = sb("dst_in_group", [P, TILES])
        REL_P, _ = sb("dst_in_pair", [P, TILES])
        FROM_LOW, _ = sb("from_low", [P, PAIRS + GROUPS])
        BELOW_LOW, _ = sb("below_low", [P, PAIRS + GROUPS])
        RANGE, _ = sb("tile_range", [1, R_WORDS * (PAIRS + GROUPS)], I32)
        IDX, _ = sb("gather_index", [P, RING, 4], I32)
        ONEHOT, _ = sb("onehot", [P, 2, P])
        XHOT, _ = sb("onehot_extra", [P, GROUP, P])
        COLS, _ = sb("cols", [P, NCOLS])
        STATS, _ = sb("stats", [P, NT, 6])
        BSTATS, _ = sb("bn_stats", [P, KH, 6 * BLOCKS])
        MV, _ = sb("bn_mean_var", [P, KH, 2])
        LN_MV, _ = sb("ln_mean_var", [P, NT, 2])
        NBIAS, _ = sb("ln_bias", [P, NT])
        RSTD, _ = sb("rstd", [P, NT])
        TMP, _ = sb("tmp", [P, 5, NT])
        SCALE, _ = sb("bn_scale", [P, KH])
        SHIFT, _ = sb("bn_shift", [P, KH])
        EPS1, _ = sb("eps1", [P, 1])
        CONST, _ = sb("consts", [P, 2])
        PLACE, _ = sb("partition", [P, 1])
        iota_at = place[0]
        IOTA, _ = sb("iota", [P, NP])
        W4, at = sb("w4", [P, KD, DIM], at=iota_at)
        XWORK_0, at = sb("mish3_work_0", [P, 2, BW], at=at)
        XWORK_1, _ = sb("mish3_work_1", [P, 2, BW], at=b2_at)
        XWORK = (XWORK_0[:, :, :], XWORK_1[:, :, :])
        assert max(place[0], at) <= nc.sbuf_usable_end
        ROWS0, at = sb("gather_h", [P, RING, GROUP, DIM], at=t1_at)
        HOT0, at = sb("onehot_0", [P, RING, GROUP, P], at=at)
        DST_P, at = sb("dst_pairs", [PAIRS, 2 * P], I32, at=at)
        DST_G, at = sb("dst_groups", [GROUPS, GROUP * P], I32, at=at)
        RNG_P, at = sb("range_pairs", [PAIRS, R_WORDS], I32, at=at)
        RNG_G, at = sb("range_groups", [GROUPS, R_WORDS], I32, at=at)
        LOHI, at = sb("lowest_highest", [P, 2, 2], I32, at=at)
        MULTI, at = sb("past_window", [P, 2, 1], I32, at=at)
        RANGES_I, at = sb("ranges_int", [P, PAIRS + GROUPS, R_WORDS], I32, at=at)
        RANGES, at = sb("ranges", [P, PAIRS + GROUPS, R_WORDS], at=at)
        WINDOW, at = sb("in_window", [P, PAIRS + GROUPS], at=at)
        DSTF, at = sb("dst_f", [P, TILES], at=at)
        NEXT_P, at = sb("in_next_p", [P, TILES], at=at)
        NEXT_G, at = sb("in_next_g", [P, TILES], at=at)
        assert at <= h1t_at + 4 * KH * NP
        W2_RAW, WE_RAW = AGG[:, 0:KD, :], AGG[:, KD, :]
        W01_LO, _ = sb("w01_lo", [P, KD, HID0], F32R, at=wa_at)
        W01_HI, at = sb("w01_hi", [P, KD, HID0], F32R, at=w2_at)
        assert at <= w2_end
        W02_LO, _ = sb("w02_lo", [P, KH, DIM], F32R, at=wb_at)
        W02_HI, at = sb("w02_hi", [P, KH, DIM], F32R, at=agg_at)
        assert at <= t1_at
        Z0_HI, _ = sb("z0_t_hi", [P, KD, NP], F32R, at=t1_at)
        Z0_LO, _ = sb("z0_t_lo", [P, KD, NP], F32R, at=h_at)
        H1_LO, _ = sb("hidden_lo", [P, KH, NP], F32R, at=h1t_at)
        H1_HIGHS = [sb(f"hidden_hi_{n}", [P, KH // 2, NP], F32R, at=at)[0] for n, at in enumerate((h_at, w2_at))]
        assert w2_at + 4 * KH // 2 * NP <= w2_end

        def hidden_hi(k):
            return H1_HIGHS[k // (KH // 2)][:, k % (KH // 2), :]

        HT_HI, _ = sb("h_t_hi", [P, KD, NP], F32R, at=t1_at)
        HT_LO, _ = sb("h_t_lo", [P, KD, NP], F32R, at=h1t_at + 4 * KD * NP)
        W1_LO, _ = sb("w1_lo", [P, 2 * KD, DIM], F32R, at=wa_at)
        W1_HI, _ = sb("w1_hi", [P, 2 * KD, DIM], F32R, at=wb_at)
        PST, _ = sb("p_stage", [P, NT, DIM], at=h1t_at)
        EA, at = sb("mish1_work", [P, KD, PW], at=t1_at)
        EB, at = sb("mish2_work", [P, 2, DIM], at=at)
        HF, at = sb("h_full", [P, KD, PW], at=at)
        MSG, at = sb("message", [P, 2, DIM], at=at)
        assert at <= h1t_at
        GP, at = sb("gather_pq", [P, 2 * SLOTS, DIM], at=h1t_at)
        AT_RAW, at = sb("edge_attr", [P, 2, PW], at=at)
        AT_R, at = sb("edge_attr_parts", [P, 2, PW], F32R, at=at)
        assert at <= h1t_at + 4 * KD * NP
        H_HI, at = sb("h_hi", [P, 2, KD, PW], F32R, at=h1t_at + 4 * KD * NP)
        H_LO, at = sb("h_lo", [P, 2, KD, PW], F32R, at=at)
        assert at <= h1t_at + 4 * KH * NP
        HN_HI, _ = sb("hn_t_hi", [P, KD, NP], F32R, at=t1_at)
        HN_LO, _ = sb("hn_t_lo", [P, KD, NP], F32R, at=h1t_at)
        AG_HI, _ = sb("agg_t_hi", [P, KD, NP], F32R, at=h1t_at + 4 * KD * NP)
        AG_LO, at = sb("agg_t_lo", [P, KD, NP], F32R, at=w2_at)
        assert at <= w2_end
        W3_HI, _ = sb("w3_hi", [P, 2 * KD, DIM], F32R, at=wa_at)
        W3_LO, _ = sb("w3_lo", [P, 2 * KD, DIM], F32R, at=wb_at)
        UT, _ = sb("u_t", [P, KD, NP], at=agg_at)

        BANKS = ctx.enter_context(nc.psum_tensor("banks", [P, 8, 512], F32))
        Z1, SEG, Z2 = BANKS[:, 0:2, :], BANKS[:, 2:4, :], BANKS[:, 4:8, :]
        TR = BANKS[:, 0:4, :]
        Z1v = Z1[:, :, :].rearrange("p b (c e) -> p (b c) e", c=2)

        h_tab = nc.dram_tensor("h_table", [NP, DIM], F32)
        p_tab = nc.dram_tensor("p_table", [NP, DIM], F32)
        q_tab = nc.dram_tensor("q_table", [NP, DIM], F32)
        r_tab = nc.dram_tensor("range_table", [PAIRS + GROUPS, R_WORDS], I32)

        def sem(name):
            return ctx.enter_context(nc.semaphore(name))

        idx_in, small_in, w01_in, w02_in = (sem(n) for n in ("idx_in", "small_in", "w01_in", "w02_in"))
        x_in = [sem(f"x_in{g}") for g in range(LG)]
        split_in, w1_in, w3_in, w4_in = (sem(n) for n in ("split_in", "w1_in", "w3_in", "w4_in"))
        range_out, range_in, ranges_in, range_ready = (sem(n) for n in
            ("range_out", "range_in", "ranges_in", "range_ready"))
        pool_const, dve_const, dve_chain = (sem(n) for n in ("pool_const", "dve_const", "dve_chain"))
        var_ready, std_ready, h_ready, h_stored = (sem(n) for n in
            ("var_ready", "std_ready", "h_ready", "h_stored"))
        norm_done, scale_ready, drow_in, r2_moved, rows_in = (sem(n) for n in
            ("norm_done", "scale_ready", "drow_in", "r2_moved", "rows_in"))
        idx_copied = sem("idx_copied")
        gat0 = [sem(f"gathered0_{g}") for g in range(RING)]
        gat1 = [sem(f"gathered1_{j}") for j in range(SLOTS)]
        hot_ready, seg_done, agg_done = sem("hot_ready"), sem("seg_done"), sem("agg_done")
        xhot_ready, xseg_done, xagg_done = sem("xhot_ready"), sem("xseg_done"), sem("xagg_done")
        tr_done = sem("tr_done")
        w3_hi, w3_lo, ag_hi, ag_lo, hn_hi, hn_lo = (sem(n) for n in
            ("w3_hi_made", "w3_lo_made", "ag_hi_made", "ag_lo_made", "hn_hi_made", "hn_lo_made"))
        mm_done, mm_moved = sem("mm_done"), sem("mm_moved")
        bn_ready, bn_applied = sem("bn_ready"), sem("bn_applied")
        w01_hi, w01_lo, w02_hi, w02_lo, w1_hi, w1_lo = (sem(n) for n in
            ("w01_hi_made", "w01_lo_made", "w02_hi_made", "w02_lo_made", "w1_hi_made", "w1_lo_made"))
        z0_hi, z0_lo, h1_hi, h1_lo, ht_hi, ht_lo = (sem(n) for n in
            ("z0_hi_made", "z0_lo_made", "h1_hi_made", "h1_lo_made", "ht_hi_made", "ht_lo_made"))
        q_moved, p_stored, q_stored = sem("q_moved"), sem("p_stored"), sem("q_stored")
        attr_in = [sem(f"attr_in{j}") for j in range(2)]
        attr_hi, attr_ready = sem("attr_hi"), sem("attr_ready")
        z1_done, a_exp, a_cut, a_sq, a_ln, a_r, h_full, h_hi, h_lo = ([sem(f"{n}_{h}") for h in range(2)] for n in
            ("z1_done", "a_exp", "a_cut", "a_sq", "a_ln", "a_r", "h_full", "h_hi", "h_lo"))
        z2_done = sem("z2_done")
        b_exp, b_cut, b_sq, b_ln, b_r, msg_ready = (sem(n) for n in
            ("b_exp", "b_cut", "b_sq", "b_ln", "b_r", "msg_ready"))
        u_bias, u_exp, u_cut, u_sq, u_ln, u_r, u_ready = (sem(n) for n in
            ("u_bias", "u_exp", "u_cut", "u_sq", "u_ln", "u_r", "u_ready"))
        y_done, y_moved, out_ready, out_stored = (sem(n) for n in
            ("y_done", "y_moved", "out_ready", "out_stored"))

        block = ctx.enter_context(nc.Block())

        def range_words(row, word, n):
            return RANGE[0:1, bass.ds(R_WORDS * row + word, n)]

        TR_R2 = NT
        VAR_BN1 = LG
        VAR_BN2 = VAR_BN1 + KH
        VAR_LN2 = VAR_BN2 + KD
        VAR_LN3 = VAR_LN2 + LG
        SUMS0, SUMS1 = 1, GROUPS + 2
        XBANK = 4
        MM_1 = 0
        FREE = 4
        MM_2 = BLOCKS * KH
        MM_PQ = MM_2 + BLOCKS * KD
        H_STORED, TABLE_STORED = 16 * LG, 16 * NT

        @block.sync
        def _(sp):
            sp.dma_start(DST_P[:, :], dst_rows.rearrange("(s t) e -> s (t e)", t=2)).then_inc(drow_in, 16)
            sp.dma_start(DST_G[:, :], dst_rows.rearrange("(g t) e -> g (t e)", t=GROUP)).then_inc(drow_in, 16)
            for g, (a, b) in enumerate(LN_GROUPS):
                sp.dma_start(X[:, a:b, :], x[a * P:b * P, :].rearrange("(t p) d -> p t d", p=P)).then_inc(x_in[g], 16)
            sp.dma_start(SRC[:, :], src_cols).then_inc(idx_in, 16)
            sp.dma_start(DST[:, :], dst_cols).then_inc(idx_in, 16)
            sp.dma_start(COLS[:, :], cols).then_inc(small_in, 16)
            sp.dma_start(EPS1[:, :], eps.partition_broadcast(P)).then_inc(small_in, 16)
            sp.wait_ge(range_ready, 2)
            sp.dma_start(r_tab[0:PAIRS, :], RNG_P[:, :]).then_inc(range_out, 16)
            sp.dma_start(r_tab[PAIRS:, :], RNG_G[:, :]).then_inc(range_out, 16)
            sp.wait_ge(range_out, 32)
            sp.dma_start(RANGE[0:1, :], r_tab.rearrange("(o s) j -> o (s j)", o=1)).then_inc(range_in, 16)
            sp.dma_start(RANGES_I[:, :, :], r_tab[:, :].partition_broadcast(P)).then_inc(ranges_in, 16)
            for a, b in LN_GROUPS:
                sp.wait_ge(h_ready, b)
                sp.dma_start(h_tab[a * P:b * P, :].rearrange("(t p) d -> p t d", p=P), H[:, a:b, :]).then_inc(h_stored, 16)
            for c in range(KD):
                sp.wait_ge(agg_done, SUMS0 + RING + 2 * c)
                sp.dma_start(WA0[:, c, :], w01[c * P:(c + 1) * P, :]).then_inc(w01_in, 16)
            for c in range(KD):
                sp.wait_ge(agg_done, SUMS0 + RING + 2 * (KD + c))
                sp.dma_start(WB[:, 2 * c:2 * c + 2, :], w02[2 * c * P:2 * (c + 1) * P, :].rearrange("(k p) n -> p k n", p=P)).then_inc(w02_in, 16)
            sp.wait_ge(agg_done, SUMS0 + RING + 4 * KD)
            sp.dma_start(ROWS[:, :, :], rows.partition_broadcast(P)).then_inc(rows_in, 16)
            sp.wait_ge(mm_done, MM_2)
            sp.dma_start(WA[:, :, :], w1[0:2 * DIM, :].rearrange("(k p) n -> p k n", p=P)).then_inc(w1_in, 16)
            sp.wait_ge(mm_done, MM_PQ)
            sp.dma_start(W2_RAW, w2.rearrange("(k p) n -> p k n", p=P)).then_inc(split_in, 16)
            for half in range(2):
                sp.dma_start(WE_RAW[EDGE_DIM * half:EDGE_DIM * (half + 1), :], w1[2 * DIM:, :]).then_inc(split_in, 16)
            for nt in range(NT):
                sp.wait_ge(mm_moved, FREE + MM_PQ + nt + 1)
                sp.dma_start(p_tab[nt * P:(nt + 1) * P, :], PST[:, nt, :]).then_inc(p_stored, 16)
            sp.wait_ge(p_stored, TABLE_STORED)
            for j in range(2):
                sp.dma_start(AT_RAW[:, j, :], edge_attr_t[j, :, :]).then_inc(attr_in[j], 16)
            for nt in range(NT):
                sp.wait_ge(q_moved, nt + 1)
                sp.dma_start(q_tab[nt * P:(nt + 1) * P, :], AGG[:, nt, :]).then_inc(q_stored, 16)

            def attributes(i, pairs=2):
                for j in range(pairs):
                    sp.wait_ge(attr_ready, 2 * i + j - 1)
                    sp.dma_start(AT_RAW[:, j, :], edge_attr_t[bass.ds(2 * i + j, 1), :, :]
                                 .rearrange("o p e -> (o p) e")).then_inc(attr_in[j], 16)

            with sp.Fori(1, 1 + 2 * KD) as i:
                attributes(i)
                sp.dma_start(WB[:, bass.ds(i - 1, 1), :].rearrange("p o n -> p (o n)"),
                             w3[bass.ds((i - 1) * P, P), :]).then_inc(w3_in, 16)
            with sp.Fori(1 + 2 * KD, EDGE_PAIRS // 2) as i:
                attributes(i)
            attributes(EDGE_PAIRS // 2, EDGE_PAIRS % 2)
            sp.wait_ge(tr_done, 3 * NT + 1)
            sp.dma_start(W4[:, :, :], w4.rearrange("(k p) n -> p k n", p=P)).then_inc(w4_in, 16)
            for nt in range(NT):
                n = min(P, NODES - nt * P)
                sp.wait_ge(out_ready, nt + 1)
                sp.dma_start(out[nt * P:nt * P + n, :], H[0:n, nt, :]).then_inc(out_stored, 16)
            sp.wait_ge(out_stored, 16 * NT)

        @block.gpsimd
        def _(pool):
            nc.gpsimd.memset(IDENT[:, :], 0.0).then_inc(pool_const, 1)
            nc.gpsimd.iota(IOTA[:, :], [[1, NP]], base=0, channel_multiplier=0,
                           allow_small_or_imprecise_dtypes=True).then_inc(pool_const, 1)
            pool.wait_ge(pool_const, 2)
            nc.gpsimd.affine_select(out=IDENT[:, :], in_=IDENT[:, :], compare_op=ALU.not_equal, fill=1.0,
                                    base=0, pattern=[[-1, P]], channel_multiplier=1).then_inc(pool_const, 1)
            nc.gpsimd.iota(PLACE[:, :], [[0, 1]], base=0, channel_multiplier=1,
                           allow_small_or_imprecise_dtypes=True).then_inc(pool_const, 1)
            pool.wait_ge(idx_in, 32)
            held = [pool.alloc_register(f"pool_held{n}") for n in range(2)]

            def reached(n, value):
                if isinstance(value, int):
                    return value
                pool.reg_mov(held[n], value)
                return pool.snap(held[n])

            pool.wait_ge(h_stored, H_STORED)

            def gather0(i, first):
                for g in range(RING):
                    n = RING * i + g
                    summed, copied = reached(0, SUMS0 + n - RING + 1), reached(1, n + 1)
                    pool.wait_ge(idx_in, 32)
                    if not first:
                        pool.wait_ge(agg_done, summed)
                    nc.gpsimd.tensor_copy(IDX[:, g, :], SRC[:, bass.ds(GROUP * n, GROUP)]).then_inc(idx_copied, 1)
                    pool.wait_ge(h_stored, H_STORED)
                    pool.wait_ge(idx_copied, copied)
                    for j in range(GROUP):
                        nc.gpsimd.indirect_dma_start(
                            ROWS0[:, g, j, :], None, h_tab[:, :],
                            bass.IndirectOffsetOnAxis(ap=IDX[:, g, j:j + 1], axis=0)).then_inc(gat0[g], 16)

            gather0(0, True)
            with pool.Fori(1, GROUPS // RING) as i:
                gather0(i, False)

            pool.wait_ge(w02_in, 16 * KD)
            pool.wait_ge(tr_done, NT)
            nc.gpsimd.tensor_copy(W02_HI[:, :, :], WB[:, :, :]).then_inc(w02_hi, 1)
            pool.wait_ge(w02_hi, 1)
            nc.gpsimd.tensor_tensor(W02_LO[:, :, :], WB[:, :, :], W02_HI[:, :, :].bitcast(F32), ALU.subtract).then_inc(w02_lo, 1)
            pool.wait_ge(w1_hi, 1)
            nc.gpsimd.tensor_tensor(W1_LO[:, :, :], WA[:, :, :], W1_HI[:, :, :].bitcast(F32), ALU.subtract).then_inc(w1_lo, 1)

            pool.wait_ge(agg_done, SUMS0 + GROUPS)

            def gather_p(i, j):
                s = SLOTS * i + j
                in_psum, copied = reached(0, s - SLOTS + 1), reached(1, GROUPS + 2 * (s + 1))
                pool.wait_ge(idx_in, 32)
                if not isinstance(s, int) or s >= SLOTS:
                    pool.wait_ge(z1_done[1], in_psum)
                nc.gpsimd.tensor_copy(IDX[:, j, 0:2], SRC[:, bass.ds(2 * s, 2)]).then_inc(idx_copied, 1)
                nc.gpsimd.tensor_copy(IDX[:, j, 2:4], DST[:, bass.ds(2 * s, 2)]).then_inc(idx_copied, 1)
                pool.wait_ge(p_stored, TABLE_STORED)
                pool.wait_ge(idx_copied, copied)
                for k in range(2):
                    nc.gpsimd.indirect_dma_start(
                        GP[:, 2 * j + k, :], None, p_tab[:, :],
                        bass.IndirectOffsetOnAxis(ap=IDX[:, j, k:k + 1], axis=0)).then_inc(gat1[j], 16)

            def gather_q(i, j):
                p_rows = reached(0, 64 * i + 32)
                pool.wait_ge(q_stored, TABLE_STORED)
                pool.wait_ge(gat1[j], p_rows)
                for k in range(2):
                    nc.gpsimd.indirect_dma_start(
                        GP[:, 2 * j + k, :], None, q_tab[:, :],
                        bass.IndirectOffsetOnAxis(ap=IDX[:, j, 2 + k:3 + k], axis=0),
                        compute_op=ALU.add).then_inc(gat1[j], 16)

            for j in range(SLOTS):
                gather_p(0, j)
            for j in range(SLOTS - 1):
                gather_q(0, j)
            def gathers(i, slots):
                for j in range(slots):
                    gather_p(i, j)
                    gather_q(i - (j == 0), (j - 1) % SLOTS)

            with pool.Fori(1, EDGE_PAIRS // SLOTS) as i:
                gathers(i, SLOTS)
            gathers(EDGE_PAIRS // SLOTS, EDGE_PAIRS % SLOTS)
            gather_q((EDGE_PAIRS - 1) // SLOTS, (EDGE_PAIRS - 1) % SLOTS)

        @block.tensor
        def _(pe):
            extras = pe.alloc_register("pe_extras")
            pe.reg_mov(extras, 1)
            more = pe.alloc_register("pe_more")

            def load_extra(row):
                pe.load(more, range_words(row, R_EXTRA, 1))
                return pe.snap(more, min_val=0, max_val=NT - 1)

            def segment_sum(bank, hots, rows):
                for j, (hot, row) in enumerate(zip(hots, rows)):
                    mm = pe.matmul(bank, hot, row, start=(j == 0), stop=(j == len(hots) - 1))
                return mm

            def extra_tiles(more_tiles, bank, rows):
                with pe.If(more_tiles > 0):
                    with pe.Fori(0, more_tiles) as _:
                        n = pe.snap(extras)
                        pe.wait_ge(xagg_done, n)
                        pe.wait_ge(xhot_ready, n + 1)
                        segment_sum(bank, [XHOT[:, j, :] for j in range(len(rows))], rows).then_inc(xseg_done, 1)
                        pe.reg_add(extras, extras, 1)

            pe.wait_ge(range_in, 16)

            def rows0(g):
                return [ROWS0[:, g, j, :] for j in range(GROUP)]

            def segment0(i, g):
                n = RING * i + g
                pe.wait_ge(gat0[g], 16 * GROUP * (i + 1))
                pe.wait_ge(hot_ready, n + 1)
                segment_sum(BANKS[:, g, :], [HOT0[:, g, j, :] for j in range(GROUP)], rows0(g)).then_inc(seg_done, 1)

            def groups0(i, last):
                for g in range(RING):
                    more_tiles = load_extra(PAIRS + RING * i + g)
                    if not last or g < RING - 1:
                        segment0(i + (g + 1) // RING, (g + 1) % RING)
                    extra_tiles(more_tiles, BANKS[:, XBANK, :], rows0(g))

            segment0(0, 0)
            with pe.Fori(0, GROUPS // RING - 1) as i:
                groups0(i, False)
            groups0(GROUPS // RING - 1, True)

            freed = []

            def transposes(source, ready, count, moved, base, back=False):
                for nt in range(NT):
                    n = len(freed)
                    pe.wait_ge(ready, count(nt))
                    if n >= 4:
                        pe.wait_ge(*freed[n - 4])
                    for c in range(KD):
                        view = source[:, c, nt * P:(nt + 1) * P] if back else source[:, nt, c * P:(c + 1) * P]
                        mm = pe.transpose(TR[:, n % 4, c * P:(c + 1) * P], view, IDENT[:, :])
                    mm.then_inc(tr_done, 1)
                    freed.append((moved, base + nt + 1))

            def product_t(base, weights, acts, kn, on, ready, count):
                def terms(k, o, b):
                    bank = Z2[:, bass.ds(b, 1), 0:BW].rearrange("p o n -> p (o n)")
                    nodes = bass.ds(b * BW, BW)
                    for n, (w, a) in enumerate(((0, 1), (1, 0), (0, 0))):
                        mm = pe.matmul(bank, weights[w][:, k, o * P:(o + 1) * P], acts[a](k)[:, nodes],
                                       start=(k == 0 and n == 0), stop=(k == kn - 1 and n == 2), skip_group_check=True)
                    return mm

                for k in range(kn):
                    pe.wait_ge(ready, count(k))
                    for b in range(BLOCKS):
                        if k == 0:
                            pe.wait_ge(mm_moved, base + b + 1)
                        mm = terms(k, 0, b)
                        if k == kn - 1:
                            mm.then_inc(mm_done, 1)
                for o in range(1, on):
                    with pe.Fori(0, BLOCKS) as b:
                        pe.wait_ge(mm_moved, base + BLOCKS * o + b + 1)
                        for k in range(kn):
                            mm = terms(k, o, b)
                        mm.then_inc(mm_done, 1)

            pe.wait_ge(pool_const, 3)
            transposes(AGG, agg_done, lambda nt: SUMS0 + GROUPS, z0_lo, 0)
            pe.wait_ge(w01_lo, KD)
            product_t(MM_1, (W01_HI, W01_LO), (lambda k: Z0_HI[:, k, :], lambda k: Z0_LO[:, k, :]), KD, KH,
                      z0_lo, lambda k: NT)
            pe.wait_ge(w02_lo, 1)
            product_t(MM_2, (W02_HI, W02_LO), (hidden_hi, lambda k: H1_LO[:, k, :]), KH, KD,
                      h1_lo, lambda k: k + 1)
            transposes(T1, bn_applied, lambda nt: KH + KD, r2_moved, 0, back=True)
            transposes(H, h_ready, lambda nt: NT + nt + 1, ht_lo, 0)

            pe.wait_ge(w1_lo, 1)
            for part, moved, base in ((0, mm_moved, FREE + MM_PQ), (1, q_moved, 0)):
                for nt in range(NT):
                    pe.wait_ge(ht_lo, nt + 1)
                    if nt >= 2:
                        pe.wait_ge(moved, base + nt - 1)
                    for k in range(KD):
                        for a, w in ((HT_LO, W1_HI), (HT_HI, W1_LO), (HT_HI, W1_HI)):
                            mm = pe.matmul(Z2[:, 2 * part + nt % 2, :], a[:, k, nt * P:(nt + 1) * P], w[:, KD * part + k, :],
                                           start=(k == 0 and a is HT_LO), stop=(k == KD - 1 and a is HT_HI and w is W1_HI))
                    mm.then_inc(mm_done, 1)
            pe.wait_ge(mm_moved, FREE + MM_PQ + NT)
            pe.wait_ge(q_moved, NT)

            def z1(i, j):
                s = SLOTS * i + j
                pe.wait_ge(gat1[j], 64 * (i + 1))
                for b in range(2):
                    if not (isinstance(s, int) and s == 0):
                        pe.wait_ge(h_full[b], s)
                    for c in (2 * b, 2 * b + 1):
                        for k in range(2):
                            pe.matmul(Z1v[:, c, k * P:(k + 1) * P], GP[:, 2 * j + k, c * P:(c + 1) * P],
                                      IDENT[:, :], is_transpose=True, skip_group_check=True,
                                      start=(c == 2 * b and k == 0), stop=False)
                    pe.wait_ge(attr_ready, s + 1)
                    for c in (2 * b, 2 * b + 1):
                        for w in (WE_HI, WE_LO):
                            mm = pe.matmul(Z1v[:, c, :], w[:, c * P:(c + 1) * P], AT_R[:, j % 2, :],
                                           skip_group_check=True, start=False, stop=(w is WE_LO and c == 2 * b + 1))
                    mm.then_inc(z1_done[b], 1)

            def z2(s, j, k):
                if k == 0:
                    if not isinstance(s, int) or s >= 2:
                        pe.wait_ge(msg_ready, 1 + s - 1)
                    pe.wait_ge(h_lo[0], s + 1)
                    pe.wait_ge(h_lo[1], s + 1)
                at = Z2[:, 2 * j + k, :]
                pe.matmul(at, ONES_R[:, :], B2_R[:, :], start=True, stop=False)
                for c in range(KD):
                    e = slice(k * P, (k + 1) * P)
                    pe.matmul(at, H_LO[:, j, c, e], W2_HI[:, c, :], start=False, stop=False)
                    pe.matmul(at, H_HI[:, j, c, e], W2_LO[:, c, :], start=False, stop=False)
                    mm = pe.matmul(at, H_HI[:, j, c, e], W2_HI[:, c, :], start=False, stop=(c == KD - 1))
                if k == 1:
                    mm.then_inc(z2_done, 1)

            def segment1(s):
                pe.wait_ge(msg_ready, 1 + s + 1)
                segment_sum(SEG[:, 0, :], [ONEHOT[:, j, :] for j in range(2)], [MSG[:, j, :] for j in range(2)]).then_inc(seg_done, 1)

            def extras1(more_tiles):
                extra_tiles(more_tiles, SEG[:, 1, :], [MSG[:, j, :] for j in range(2)])

            def edge_step(i, j, first):
                s = SLOTS * i + j
                if not first:
                    more_tiles = load_extra(s - 3)
                z1(i, j)
                z2(s - 1, (j - 1) % 2, 0)
                if not first:
                    extras1(more_tiles)
                z2(s - 1, (j - 1) % 2, 1)
                segment1(s - 2)

            z1(0, 0)
            z1(0, 1)
            for k in range(2):
                z2(0, 0, k)
            for j in range(2, SLOTS):
                edge_step(0, j, j == 2)
            with pe.Fori(1, EDGE_PAIRS // SLOTS) as i:
                for j in range(SLOTS):
                    edge_step(i, j, False)
            for j in range(EDGE_PAIRS % SLOTS):
                edge_step(EDGE_PAIRS // SLOTS, j, False)
            more_tiles = load_extra(EDGE_PAIRS - 3)
            extras1(more_tiles)
            for k in range(2):
                z2(EDGE_PAIRS - 1, (EDGE_PAIRS - 1) % 2, k)
            for s in (EDGE_PAIRS - 2, EDGE_PAIRS - 1):
                segment1(s)
                extras1(load_extra(s))

            extra_sums = pe.snap(extras)
            pe.wait_ge(xagg_done, extra_sums)
            transposes(AGG, agg_done, lambda nt: SUMS1 + EDGE_PAIRS, ag_lo, 0)
            transposes(H, h_ready, lambda nt: 2 * NT, hn_lo, 0)
            pe.wait_ge(w3_lo, KD)
            pe.wait_ge(ag_lo, NT)
            pe.wait_ge(hn_lo, NT)
            with pe.Fori(0, BLOCKS) as b:
                for o in range(KD):
                    pe.wait_ge(u_ready, UPAIRS * b + o // 2 + 1)
                    for k in range(2 * KD):
                        high, low = (HN_HI, HN_LO) if k < KD else (AG_HI, AG_LO)
                        for n, (w, a) in enumerate(((W3_HI, low), (W3_LO, high), (W3_HI, high))):
                            mm = pe.matmul(Z2[:, o, 0:BW], w[:, k, o * P:(o + 1) * P], a[:, k % KD, bass.ds(b * BW, BW)],
                                           start=(k == 0 and n == 0), stop=(k == 2 * KD - 1 and n == 2))
                    mm.then_inc(mm_done, 1)
            pe.wait_ge(w4_in, 16)
            for nt in range(NT):
                pe.wait_ge(u_ready, UPAIRS + UPAIRS * (((nt + 1) * P - 1) // BW + 1))
                if nt >= 2:
                    pe.wait_ge(y_moved, nt - 1)
                for k in range(KD):
                    mm = pe.matmul(SEG[:, nt % 2, :], UT[:, k, nt * P:(nt + 1) * P], W4[:, k, :],
                                   start=(k == 0), stop=(k == KD - 1))
                mm.then_inc(y_done, 1)

        @block.scalar
        def _(act):
            def normalise(target, source, func, base, done):
                for g, (a, b) in enumerate(LN_GROUPS):
                    act.wait_ge(var_ready, base + g + 1)
                    nc.scalar.activation(TMP[:, 4, a:b], LN_MV[:, a:b, 1], ACT.Sqrt, bias=CONST[:, 1:2]).then_inc(std_ready, 1)
                    act.wait_ge(scale_ready, ln_groups[0] + 1)
                    ln_groups[0] += 1
                    for nt in range(a, b):
                        nc.scalar.activation(target[:, nt, :], source[:, nt, :], func, bias=NBIAS[:, nt:nt + 1],
                                             scale=RSTD[:, nt:nt + 1]).then_inc(done, 1)

            ln_groups = [0]
            def move_hi(target, base, done, scale=1.0):
                for nt in range(NT):
                    act.wait_ge(tr_done, base + nt + 1)
                    nc.scalar.mul(target[:, :, nt * P:(nt + 1) * P],
                                  TR[:, (base + nt) % 4, :].rearrange("p (c e) -> p c e", c=KD), scale).then_inc(done, 1)

            def move_product(base, target, on, bias, var):
                def std(o):
                    act.wait_ge(var_ready, var + o + 1)
                    nc.scalar.activation(TMP[:, 3, o:o + 1], MV[:, o, 1:2], ACT.Sqrt, bias=CONST[:, 1:2]).then_inc(std_ready, 1)

                def apply(o):
                    act.wait_ge(bn_ready, var - VAR_BN1 + o + 1)
                    nc.scalar.activation(target[:, o, :], target[:, o, :], ACT.Relu, bias=SHIFT[:, o:o + 1],
                                         scale=SCALE[:, o:o + 1]).then_inc(bn_applied, 1)

                for o in range(on):
                    for b in range(BLOCKS):
                        act.wait_ge(mm_done, base + BLOCKS * o + b + 1)
                        nc.scalar.activation(target[:, o, b * BW:(b + 1) * BW], Z2[:, b, 0:BW], ACT.Identity,
                                             bias=COLS[:, bias + o:bias + o + 1]).then_inc(mm_moved, 1)
                        if o > 0 and b == 0:
                            std(o - 1)
                        if o > 0 and b == 1:
                            apply(o - 1)
                return lambda: std(on - 1), lambda: apply(on - 1)

            act.wait_ge(dve_const, 1)
            normalise(H, X, ACT.Relu, 0, h_ready)
            act.wait_ge(small_in, 32)
            act.wait_ge(w01_in, 16 * KD)
            for c in range(KD):
                nc.scalar.copy(W01_HI[:, c, :], WA0[:, c, :]).then_inc(w01_hi, 1)
            move_hi(Z0_HI, 0, z0_hi)
            last_std, last_apply = move_product(MM_1, H1T, KH, CB1, VAR_BN1)
            last_std()
            act.wait_ge(mm_done, MM_2)
            for k in range(KH):
                act.wait_ge(bn_applied, k + 1)
                nc.scalar.copy(hidden_hi(k), H1T[:, k, :]).then_inc(h1_hi, 1)
                if k == 0:
                    last_apply()
            last_std, last_apply = move_product(MM_2, T1, KD, CB2, VAR_BN2)
            last_std()
            last_apply()
            act.wait_ge(h_stored, H_STORED)
            act.wait_ge(w1_in, 16)
            act.wait_ge(mm_done, MM_PQ)
            nc.scalar.copy(W1_HI[:, :, :], WA[:, :, :]).then_inc(w1_hi, 1)
            normalise(H, X, ACT.Relu, VAR_LN2, h_ready)
            move_hi(HT_HI, 2 * NT, ht_hi)
            for nt in range(NT):
                act.wait_ge(mm_done, MM_PQ + nt + 1)
                nc.scalar.copy(PST[:, nt, :], Z2[:, nt % 2, :]).then_inc(mm_moved, 1)

            nc.scalar.preload_act_table_set("natural_log_exp_and_others")

            def exp1(s, h):
                act.wait_ge(z1_done[h], s + 1)
                if not (isinstance(s, int) and s == 0):
                    act.wait_ge(h_full[h], s)
                nc.scalar.activation(EA[:, 2 * h:2 * h + 2, :], Z1v[:, 2 * h:2 * h + 2, :], ACT.Exp).then_inc(a_exp[h], 1)

            def log1(s, h):
                act.wait_ge(a_sq[h], s + 1)
                nc.scalar.activation(EA[:, 2 * h:2 * h + 2, :], EA[:, 2 * h:2 * h + 2, :], ACT.Ln, bias=CONST[:, 0:1]).then_inc(a_ln[h], 1)

            def inv1(s, h):
                act.wait_ge(a_ln[h], s + 1)
                nc.scalar.activation(EA[:, 2 * h:2 * h + 2, :], EA[:, 2 * h:2 * h + 2, :], ACT.Exp, scale=-1.0).then_inc(a_r[h], 1)

            def hi1(s, j, h):
                act.wait_ge(h_full[h], s + 1)
                if not isinstance(s, int) or s >= 2:
                    act.wait_ge(z2_done, s - 1)
                nc.scalar.copy(H_HI[:, j, 2 * h:2 * h + 2, :], HF[:, 2 * h:2 * h + 2, :]).then_inc(h_hi[h], 1)

            def exp2(s, j):
                act.wait_ge(z2_done, s + 1)
                act.wait_ge(msg_ready, 1 + s)
                nc.scalar.activation(EB[:, :, :], Z2[:, 2 * j:2 * j + 2, :], ACT.Exp).then_inc(b_exp, 1)

            def sq2(s):
                act.wait_ge(b_cut, s + 1)
                nc.scalar.activation(EB[:, :, :], EB[:, :, :], ACT.Square).then_inc(b_sq, 1)

            def log2(s):
                act.wait_ge(b_sq, s + 1)
                nc.scalar.activation(EB[:, :, :], EB[:, :, :], ACT.Ln, bias=CONST[:, 0:1]).then_inc(b_ln, 1)

            def inv2(s):
                act.wait_ge(b_ln, s + 1)
                nc.scalar.activation(EB[:, :, :], EB[:, :, :], ACT.Exp, scale=-1.0).then_inc(b_r, 1)

            def attr_high(i, j):
                s = 2 * i + j
                act.wait_ge(attr_in[j], 16 * (i + 1))
                if not isinstance(s, int) or s >= 2:
                    act.wait_ge(z1_done[1], s - 1)
                nc.scalar.copy(AT_R[:, j, :], AT_RAW[:, j, :]).then_inc(attr_hi, 1)

            def mish_a(s, j):
                for h in range(2):
                    exp1(s, h)
                for h in range(2):
                    log1(s, h)
                for h in range(2):
                    inv1(s, h)
                for h in range(2):
                    hi1(s, j, h)

            def mish_b(s, j):
                exp2(s, j)
                sq2(s)
                log2(s)
                inv2(s)

            def edge_step(i, j, more):
                s = 2 * i + j
                exp2(s - 2, j)
                exp1(s, 0)
                sq2(s - 2)
                exp1(s, 1)
                log2(s - 2)
                inv2(s - 2)
                for step in (log1, inv1):
                    for h in range(2):
                        step(s, h)
                if more:
                    attr_high(i + j, 1 - j)
                for h in range(2):
                    hi1(s, j, h)

            for j in range(2):
                attr_high(0, j)
            mish_a(0, 0)
            attr_high(1, 0)
            mish_a(1, 1)
            with act.Fori(1, LAST) as i:
                for j in range(2):
                    edge_step(i, j, True)
            def w3_high(n):
                nc.scalar.copy(W3_HI[:, 2 * n:2 * n + 2, :], WB[:, 2 * n:2 * n + 2, :]).then_inc(w3_hi, 1)

            act.wait_ge(w3_in, 16 * 2 * KD)
            w3_high(0)
            for s in range(2 * LAST, EDGE_PAIRS):
                edge_step(LAST, s % 2, s < EDGE_PAIRS - 1)
            w3_high(1)
            for n, s in enumerate((EDGE_PAIRS - 2, EDGE_PAIRS - 1)):
                mish_b(s, s % 2)
                w3_high(2 + n)

            move_hi(AG_HI, 3 * NT, ag_hi, scale=-2.0)
            move_hi(HN_HI, 4 * NT, hn_hi)
            with act.Fori(0, BLOCKS) as b:
                for q in range(UPAIRS):
                    n, work = UPAIRS * b + q, XWORK[q]
                    for o in (2 * q, 2 * q + 1):
                        act.wait_ge(mm_done, MM_PQ + 2 * NT + KD * b + o + 1)
                        nc.scalar.activation(UT[:, o, bass.ds(b * BW, BW)], Z2[:, o, 0:BW], ACT.Identity,
                                             bias=COLS[:, CB3 + o:CB3 + o + 1]).then_inc(u_bias, 1)
                    act.wait_ge(u_cut, n + 1)
                    nc.scalar.activation(work, work, ACT.Exp).then_inc(u_exp, 1)
                    act.wait_ge(u_exp, n + 1)
                    nc.scalar.activation(work, work, ACT.Square, bias=CONST[:, 0:1]).then_inc(u_sq, 1)
                    act.wait_ge(u_sq, n + 1)
                    nc.scalar.activation(work, work, ACT.Ln, bias=CONST[:, 0:1]).then_inc(u_ln, 1)
                    act.wait_ge(u_ln, n + 1)
                    nc.scalar.activation(work, work, ACT.Exp, scale=-1.0).then_inc(u_r, 1)
            normalise(H, H, ACT.Identity, VAR_LN3, norm_done)

        @block.vector
        def _(dve):
            chain = [0]

            def link(ins):
                chain[0] += 1
                ins.then_inc(dve_chain, 1)
                dve.wait_ge(dve_chain, chain[0])

            extras = dve.alloc_register("dve_extras")
            dve.reg_mov(extras, 1)

            def ln_stats(source, g):
                a, b = LN_GROUPS[g]
                for nt in range(a, b):
                    nc.vector.bn_stats(STATS[:, nt, :], source[:, nt, :]).then_inc(dve_chain, 1)
                chain[0] += b - a
                for nt in range(a, b):
                    dve.wait_ge(dve_chain, chain[0] - (b - 1 - nt))
                    ins = nc.vector.bn_aggr(LN_MV[:, nt, :], STATS[:, nt, :])
                    if nt == b - 1:
                        ins.then_inc(var_ready, 1)

            def ln_scale(g, count):
                a, b = LN_GROUPS[g]
                dve.wait_ge(std_ready, count + g + 1)
                link(nc.vector.reciprocal(RSTD[:, a:b], TMP[:, 4, a:b]))
                nc.vector.scalar_tensor_tensor(NBIAS[:, a:b], LN_MV[:, a:b, 0], -1.0, RSTD[:, a:b],
                                               ALU.mult, ALU.mult).then_inc(scale_ready, 1)

            def batch_norm(source, on, gamma, beta, base, var):
                for o in range(on):
                    c = slice(o, o + 1)
                    for b, (first, end) in enumerate(BN_PIECES):
                        dve.wait_ge(mm_moved, FREE + base + BLOCKS * o + b + 1)
                        nc.vector.bn_stats(BSTATS[:, o, 6 * b:6 * b + 6], source[:, o, first:end]).then_inc(dve_chain, 1)
                        chain[0] += 1
                    dve.wait_ge(dve_chain, chain[0])
                    nc.vector.bn_aggr(MV[:, o, :], BSTATS[:, o, :]).then_inc(var_ready, 1)
                    dve.wait_ge(var_ready, var + o + 1)
                    dve.wait_ge(std_ready, var + o + 1)
                    link(nc.vector.reciprocal(TMP[:, 0, c], TMP[:, 3, c]))
                    link(nc.vector.tensor_tensor(SCALE[:, c], TMP[:, 0, c], COLS[:, gamma + o:gamma + o + 1], ALU.mult))
                    link(nc.vector.tensor_tensor(TMP[:, 1, c], MV[:, o, 0:1], SCALE[:, c], ALU.mult))
                    nc.vector.tensor_tensor(SHIFT[:, c], COLS[:, beta + o:beta + o + 1], TMP[:, 1, c], ALU.subtract).then_inc(bn_ready, 1)

            def move_lo(target, high, base, high_made, done, scale=1.0):
                for nt in range(NT):
                    dve.wait_ge(high_made, nt + 1)
                    at = slice(nt * P, (nt + 1) * P)
                    nc.vector.scalar_tensor_tensor(target[:, :, at], TR[:, (base + nt) % 4, :].rearrange("p (c e) -> p c e", c=KD),
                                                   scale, high[:, :, at].bitcast(F32), ALU.mult, ALU.subtract).then_inc(done, 1)

            range_regs = [[dve.alloc_register(f"dve_range{n}_{j}") for j in range(R_USED)] for n in range(RING)]

            def load_range(n, row):
                dve.load(range_regs[n], range_words(row, R_LOW, R_USED))

            def low_tile(n):
                return dve.snap(range_regs[n][R_LOW], min_val=0, max_val=NT - 1)

            def make_hots(hots, rel, tile, past=0):
                for j, at in enumerate(hots):
                    ins = nc.vector.tensor_scalar(at, IOTA[:, bass.ds(past * P, P)], rel[:, bass.ds(tile + j, 1)], None, ALU.is_equal)
                return ins

            def node_tile(nt):
                return AGG[:, bass.ds(nt, 1), :].rearrange("p o d -> p (o d)")

            def add_sums(n, row, bank):
                next_tile = dve.snap(range_regs[n][R_NEXT], min_val=0, max_val=NT - 1)
                for nt, where in ((low_tile(n), FROM_LOW), (next_tile, BELOW_LOW)):
                    at = node_tile(nt)
                    ins = nc.vector.scalar_tensor_tensor(at, bank, where[:, bass.ds(row, 1)], at, ALU.mult, ALU.add)
                return ins

            def sums_extra(n, rel, tile, tiles, bank, added):
                past = dve.snap(range_regs[n][R_EXTRA], min_val=0, max_val=NT - 1)
                with dve.If(past > 0):
                    low = low_tile(n)
                    with dve.Fori(0, past) as k:
                        dve.reg_mov(past_low, low + k + 1)
                        nt = dve.snap(past_low, min_val=0, max_val=NT - 1)
                        n_extra = dve.snap(extras)
                        dve.wait_ge(agg_done, added)
                        dve.wait_ge(xseg_done, n_extra)
                        dve.wait_ge(xagg_done, n_extra)
                        make_hots([XHOT[:, j, :] for j in range(tiles)], rel, tile, k + 1).then_inc(xhot_ready, 1)
                        dve.wait_ge(xseg_done, n_extra + 1)
                        nc.vector.tensor_tensor(node_tile(nt), node_tile(nt), bank, ALU.add).then_inc(xagg_done, 1)
                        dve.reg_add(extras, extras, 1)

            past_low = dve.alloc_register("dve_past_low")

            def wait_extras():
                extra = dve.snap(extras)
                dve.wait_ge(xagg_done, extra)

            nc.vector.memset(CONST[:, 0:1], 1.0).then_inc(dve_chain, 1)
            nc.vector.memset(B2_R[:, :].bitcast(F32), 0.0).then_inc(dve_chain, 1)
            nc.vector.memset(ONES_R[:, :].bitcast(F32), 1.0).then_inc(dve_chain, 1)
            chain[0] += 4
            for n, (start, count) in enumerate(((mm_moved, FREE), (u_ready, UPAIRS), (msg_ready, 1),
                                                (xhot_ready, 1), (xseg_done, 1), (xagg_done, 1))):
                nc.vector.memset(TMP[:, 0, n:n + 1], 0.0).then_inc(start, count)
            nc.vector.memset(CONST[:, 1:2], LN_EPS).then_inc(dve_const, 1)
            nc.vector.memset(RNG_P[:, :], 0).then_inc(dve_chain, 1)
            link(nc.vector.memset(RNG_G[:, :], 0))
            dve.wait_ge(drow_in, 32)
            tables = [(rng, LOHI[0:n, t, :], MULTI[0:n, t, :]) for t, (rng, n) in enumerate(((RNG_P, PAIRS), (RNG_G, GROUPS)))]

            def for_tables(step):
                for n, (rng, lohi, multi) in enumerate(tables):
                    for ins in step(rng, lohi, multi):
                        ins.then_inc(dve_chain, 1)
                        chain[0] += 1
                dve.wait_ge(dve_chain, chain[0])

            for (rng, lohi, multi), dst in zip(tables, (DST_P, DST_G)):
                nc.vector.tensor_reduce(lohi[:, 0:1], dst[:, :], AX.X, ALU.min).then_inc(dve_chain, 1)
                nc.vector.tensor_reduce(lohi[:, 1:2], dst[:, :], AX.X, ALU.max).then_inc(dve_chain, 1)
                chain[0] += 2
            dve.wait_ge(dve_chain, chain[0])
            tile_bits = P.bit_length() - 1
            for_tables(lambda rng, lohi, multi: (
                nc.vector.tensor_scalar(rng[:, R_LOW:R_LOW + 2], lohi, tile_bits, None, ALU.arith_shift_right),
                nc.vector.tensor_scalar(rng[:, R_WRAP:R_WRAP + 1], lohi[:, 0:1], P - 1, None, ALU.bitwise_and),
                nc.vector.tensor_tensor(multi, lohi[:, 1:2], lohi[:, 0:1], ALU.subtract)))
            for_tables(lambda rng, lohi, multi: (
                nc.vector.tensor_scalar(multi, multi, P, None, ALU.is_ge),
                nc.vector.tensor_tensor(rng[:, R_EXTRA:R_EXTRA + 1], rng[:, R_EXTRA:R_EXTRA + 1], rng[:, R_LOW:R_LOW + 1], ALU.subtract),
                nc.vector.tensor_scalar(lohi[:, 0:1], rng[:, R_LOW:R_LOW + 1], NT - 1, -2, ALU.is_equal, ALU.mult)))
            for_tables(lambda rng, lohi, multi: (
                nc.vector.scalar_tensor_tensor(rng[:, R_NEXT:R_NEXT + 1], rng[:, R_LOW:R_LOW + 1], 1, lohi[:, 0:1], ALU.add, ALU.add),
                nc.vector.tensor_tensor(rng[:, R_EXTRA:R_EXTRA + 1], rng[:, R_EXTRA:R_EXTRA + 1], multi, ALU.mult),
                nc.vector.scalar_tensor_tensor(rng[:, R_WRAP:R_WRAP + 1], multi, 0, rng[:, R_WRAP:R_WRAP + 1], ALU.is_equal, ALU.mult)))
            nc.vector.memset(TMP[:, 0, 0:1], 0.0).then_inc(range_ready, 2)
            for g in range(LG):
                dve.wait_ge(x_in[g], 16)
                ln_stats(X, g)
                if g > 0:
                    ln_scale(g - 1, 0)
            ln_scale(LG - 1, 0)
            dve.wait_ge(idx_in, 32)
            dve.wait_ge(ranges_in, 16)
            nc.vector.tensor_copy(RANGES[:, :, :], RANGES_I[:, :, :]).then_inc(dve_chain, 1)
            chain[0] += 1
            link(nc.vector.tensor_copy(DSTF[:, :], DST[:, :]))
            dve.wait_ge(pool_const, 4)
            for at, word, value, op in ((FROM_LOW, R_WRAP, PLACE[:, 0:1], ALU.is_le), (BELOW_LOW, R_WRAP, PLACE[:, 0:1], ALU.is_gt),
                                        (WINDOW, R_EXTRA, 0.0, ALU.is_equal)):
                nc.vector.tensor_scalar(at[:, :], RANGES[:, :, word], value, None, op).then_inc(dve_chain, 1)
            views = []
            for rel, nxt, first, n in ((REL_P, NEXT_P, 0, PAIRS), (REL_G, NEXT_G, PAIRS, GROUPS)):
                wide = [P, n, TILES // n]
                rel, nxt, dst = (a[:, :].rearrange("p (n t) -> p n t", n=n) for a in (rel, nxt, DSTF))
                rows = slice(first, first + n)
                views.append((rel, nxt, WINDOW[:, rows].rearrange("p (n o) -> p n o", o=1).broadcast_to(wide)))
                nc.vector.scalar_tensor_tensor(rel, RANGES[:, rows, R_LOW:R_LOW + 1].broadcast_to(wide), -float(P), dst,
                                               ALU.mult, ALU.add).then_inc(dve_chain, 1)
            chain[0] += 5
            dve.wait_ge(dve_chain, chain[0])
            for rel, nxt, window in views:
                nc.vector.scalar_tensor_tensor(nxt, rel, float(P), window, ALU.is_ge, ALU.mult).then_inc(dve_chain, 1)
            chain[0] += 2
            dve.wait_ge(dve_chain, chain[0])
            for rel, nxt, window in views:
                nc.vector.scalar_tensor_tensor(rel, nxt, -float(P), rel, ALU.mult, ALU.add).then_inc(dve_chain, 1)
            chain[0] += 2
            dve.wait_ge(dve_chain, chain[0])
            dve.wait_ge(small_in, 32)
            link(nc.vector.tensor_scalar(EPS1[:, :], EPS1[:, :], 1.0, None, ALU.add))

            dve.wait_ge(pool_const, 3)
            dve.wait_ge(range_in, 16)

            def hots0(n, g):
                load_range(g, PAIRS + n)
                make_hots([HOT0[:, g, j, :] for j in range(GROUP)], REL_G, GROUP * n).then_inc(hot_ready, 1)

            def group0(n, g, ahead):
                if ahead:
                    hots0(n + 2, (g + 2) % RING)
                sums_extra(g, REL_G, GROUP * n, GROUP, BANKS[:, XBANK, :], SUMS0 + n)
                wait_extras()
                dve.wait_ge(seg_done, n + 1)
                dve.wait_ge(agg_done, SUMS0 + n)
                add_sums(g, PAIRS + n, BANKS[:, g, :]).then_inc(agg_done, 1)

            for g in range(2):
                hots0(g, g)
            dve.wait_ge(h_ready, NT)
            nc.vector.tensor_scalar(AGG[:, :, :], H[:, :, :], EPS1[:, 0:1], None, ALU.mult).then_inc(agg_done, 1)
            link(nc.vector.tensor_tensor(X[:, :, :], X[:, :, :], H[:, :, :], ALU.add))
            with dve.Fori(0, GROUPS // RING - 1) as i:
                for g in range(RING):
                    group0(RING * i + g, g, True)
            for g in range(RING):
                group0(GROUPS - RING + g, g, g < RING - 2)
                for c in range(g * KD // RING, (g + 1) * KD // RING):
                    dve.wait_ge(w01_hi, c + 1)
                    nc.vector.tensor_tensor(W01_LO[:, c, :], WA0[:, c, :], W01_HI[:, c, :].bitcast(F32), ALU.subtract).then_inc(w01_lo, 1)
            dve.wait_ge(h_stored, H_STORED)
            move_lo(Z0_LO, Z0_HI, 0, z0_hi, z0_lo)
            batch_norm(H1T, KH, CG1, CBE1, MM_1, VAR_BN1)
            for k in range(KH):
                dve.wait_ge(h1_hi, k + 1)
                nc.vector.tensor_tensor(H1_LO[:, k, :], H1T[:, k, :], hidden_hi(k).bitcast(F32), ALU.subtract).then_inc(h1_lo, 1)
            batch_norm(T1, KD, CG2, CBE2, MM_2, VAR_BN2)
            for g, (a, b) in enumerate(LN_GROUPS):
                for nt in range(a, b):
                    dve.wait_ge(tr_done, TR_R2 + nt + 1)
                    nc.vector.tensor_tensor(X[:, nt, :], X[:, nt, :], TR[:, (TR_R2 + nt) % 4, :], ALU.add).then_inc(r2_moved, 1)
                dve.wait_ge(r2_moved, b)
                ln_stats(X, g)
                if g > 0:
                    ln_scale(g - 1, VAR_LN2)
            ln_scale(LG - 1, VAR_LN2)
            move_lo(HT_LO, HT_HI, 2 * NT, ht_hi, ht_lo)
            dve.wait_ge(split_in, 48)
            dve.wait_ge(rows_in, 16)
            link(nc.vector.tensor_scalar(W2_RAW, W2_RAW, -2.0, None, ALU.mult))
            nc.vector.tensor_copy(W2_HI[:, :, :], W2_RAW).then_inc(dve_chain, 1)
            nc.vector.tensor_copy(WE_HI[:, :], WE_RAW).then_inc(dve_chain, 1)
            nc.vector.tensor_copy(B2_R[0:1, :], ROWS[0:1, ROW_B2, :]).then_inc(dve_chain, 1)
            nc.vector.tensor_copy(B2_R[32:33, :], ROWS[32:33, ROW_B2, :]).then_inc(dve_chain, 1)
            chain[0] += 4
            dve.wait_ge(dve_chain, chain[0])
            nc.vector.tensor_tensor(W2_LO[:, :, :], W2_RAW, W2_HI[:, :, :].bitcast(F32), ALU.subtract).then_inc(dve_chain, 1)
            nc.vector.tensor_tensor(WE_LO[:, :], WE_RAW, WE_HI[:, :].bitcast(F32), ALU.subtract).then_inc(dve_chain, 1)
            nc.vector.tensor_tensor(B2_R[32:33, :], ROWS[32:33, ROW_B2, :], B2_R[32:33, :].bitcast(F32), ALU.subtract).then_inc(dve_chain, 1)
            chain[0] += 3
            dve.wait_ge(dve_chain, chain[0])
            def wide(row):
                return ROWS[:, row:row + 1, :].broadcast_to([P, NT, DIM])
            dve.wait_ge(h_ready, 2 * NT)
            link(nc.vector.tensor_tensor(X[:, :, :], X[:, :, :], wide(ROW_BETA), ALU.add))
            for nt in range(NT):
                dve.wait_ge(mm_done, MM_PQ + NT + nt + 1)
                nc.vector.tensor_tensor(AGG[:, nt, :], Z2[:, 2 + nt % 2, :], ROWS[:, ROW_B1, :], ALU.add).then_inc(q_moved, 1)

            def attr_rest(s, j):
                dve.wait_ge(attr_hi, s + 1)
                low = AT_R[EDGE_DIM:P, j, :]
                nc.vector.tensor_tensor(low, AT_RAW[EDGE_DIM:P, j, :], low.bitcast(F32), ALU.subtract).then_inc(attr_ready, 1)

            def cut1(s, h):
                dve.wait_ge(a_exp[h], s + 1)
                at = EA[:, 2 * h:2 * h + 2, :]
                nc.vector.tensor_scalar(at, at, E_MAX, 1.0, ALU.min, ALU.add).then_inc(a_cut[h], 1)

            def sq1(s, h):
                dve.wait_ge(a_cut[h], s + 1)
                at = EA[:, 2 * h:2 * h + 2, :]
                nc.vector.tensor_tensor(at, at, at, ALU.mult).then_inc(a_sq[h], 1)

            def full1(s, h):
                dve.wait_ge(a_r[h], s + 1)
                if not (isinstance(s, int) and s == 0):
                    dve.wait_ge(h_lo[h], s)
                nc.vector.scalar_tensor_tensor(HF[:, 2 * h:2 * h + 2, :].rearrange("p c e -> p (c e)"),
                                               EA[:, 2 * h:2 * h + 2, :].rearrange("p c e -> p (c e)"),
                                               -0.5, Z1[:, h, :], ALU.add, ALU.mult).then_inc(h_full[h], 1)

            def lo1(s, j, h):
                dve.wait_ge(h_hi[h], s + 1)
                c = slice(2 * h, 2 * h + 2)
                nc.vector.tensor_tensor(H_LO[:, j, c, :], HF[:, c, :], H_HI[:, j, c, :].bitcast(F32), ALU.subtract).then_inc(h_lo[h], 1)

            def cut2(s):
                dve.wait_ge(b_exp, s + 1)
                nc.vector.tensor_scalar(EB[:, :, :], EB[:, :, :], E_MAX, 1.0, ALU.min, ALU.add).then_inc(b_cut, 1)

            def hots1(s):
                make_hots([ONEHOT[:, k, :] for k in range(2)], REL_P, 2 * s).then_inc(hot_ready, 1)

            def message(s, j):
                dve.wait_ge(b_r, s + 1)
                nc.vector.scalar_tensor_tensor(MSG[:, :, :].rearrange("p k d -> p (k d)"), EB[:, :, :].rearrange("p k d -> p (k d)"),
                                               -0.5, Z2[:, 2 * j:2 * j + 2, :].rearrange("p k d -> p (k d)"),
                                               ALU.add, ALU.mult).then_inc(msg_ready, 1)

            def sums1(s, n):
                wait_extras()
                dve.wait_ge(seg_done, GROUPS + s + 1)
                dve.wait_ge(agg_done, SUMS1 + s)
                add_sums(n, s, SEG[:, 0, :]).then_inc(agg_done, 1)
                sums_extra(n, REL_P, 2 * s, 2, SEG[:, 1, :], SUMS1 + s + 1)

            def mish_a(s, j):
                for step in (cut1, sq1, full1):
                    for h in range(2):
                        step(s, h)
                for h in range(2):
                    lo1(s, j, h)

            def mish_b(s, j):
                load_range(j, s)
                cut2(s)
                sums1(s - 1, 1 - j)
                hots1(s)
                message(s, j)

            def edge_step(s, j, first, more):
                load_range(j, s - 2)
                cut2(s - 2)
                if not first:
                    sums1(s - 3, 1 - j)
                hots1(s - 2)
                for h in range(2):
                    cut1(s, h)
                    sq1(s, h)
                message(s - 2, j)
                for h in range(2):
                    full1(s, h)
                if more:
                    attr_rest(s + 1, 1 - j)
                for h in range(2):
                    lo1(s, j, h)

            for j in range(2):
                attr_rest(j, j)
            dve.wait_ge(q_stored, TABLE_STORED)
            nc.vector.memset(AGG[:, :, :], 0.0).then_inc(agg_done, 1)
            mish_a(0, 0)
            attr_rest(2, 0)
            mish_a(1, 1)
            for j in range(2):
                edge_step(2 + j, j, j == 0, True)
            with dve.Fori(2, LAST) as i:
                for j in range(2):
                    edge_step(2 * i + j, j, False, True)
            def w3_low(n):
                dve.wait_ge(w3_hi, n + 1)
                c = slice(2 * n, 2 * n + 2)
                nc.vector.tensor_tensor(W3_LO[:, c, :], WB[:, c, :], W3_HI[:, c, :].bitcast(F32), ALU.subtract).then_inc(w3_lo, 1)

            for s in range(2 * LAST, EDGE_PAIRS):
                edge_step(s, s % 2, False, s < EDGE_PAIRS - 1)
            for n, s in enumerate((EDGE_PAIRS - 2, EDGE_PAIRS - 1)):
                mish_b(s, s % 2)
                w3_low(n)
            w3_low(2)
            sums1(EDGE_PAIRS - 1, (EDGE_PAIRS - 1) % 2)
            dve.wait_ge(agg_done, SUMS1 + EDGE_PAIRS)
            w3_low(3)
            move_lo(AG_LO, AG_HI, 3 * NT, ag_hi, ag_lo, scale=-2.0)
            move_lo(HN_LO, HN_HI, 4 * NT, hn_hi, hn_lo)

            link(nc.vector.tensor_tensor(H[:, :, :], H[:, :, :], wide(ROW_B4), ALU.add))
            with dve.Fori(0, BLOCKS) as b:
                for q in range(UPAIRS):
                    n, work = UPAIRS * b + q, XWORK[q]
                    at = UT[:, 2 * q:2 * q + 2, bass.ds(b * BW, BW)]
                    dve.wait_ge(u_bias, 2 * n + 2)
                    dve.wait_ge(u_ready, UPAIRS + n - 1)
                    nc.vector.tensor_scalar(work, at, Z_MAX, None, ALU.min).then_inc(u_cut, 1)
                    dve.wait_ge(u_r, n + 1)
                    nc.vector.scalar_tensor_tensor(at, work, -0.5, at, ALU.add, ALU.mult).then_inc(u_ready, 1)
            def finish(g):
                a, b = LN_GROUPS[g]
                for nt in range(a, b):
                    dve.wait_ge(norm_done, nt + 1)
                    link(nc.vector.tensor_tensor(H[:, nt, :], H[:, nt, :], ROWS[:, ROW_GAMMA, :], ALU.mult))
                    nc.vector.tensor_tensor(H[:, nt, :], H[:, nt, :], X[:, nt, :], ALU.add).then_inc(out_ready, 1)

            for g, (a, b) in enumerate(LN_GROUPS):
                for nt in range(a, b):
                    dve.wait_ge(y_done, nt + 1)
                    nc.vector.scalar_tensor_tensor(H[:, nt, :], SEG[:, nt % 2, :], -2.0, H[:, nt, :], ALU.mult, ALU.add).then_inc(y_moved, 1)
                dve.wait_ge(y_moved, b)
                ln_stats(H, g)
                if g > 0:
                    ln_scale(g - 1, VAR_LN3)
                    finish(g - 1)
            ln_scale(LG - 1, VAR_LN3)
            finish(LG - 1)


def kernel(**inputs):
    import numpy as np
    import concourse.bacc as bacc
    from concourse.bass_utils import run_bass_kernel_spmd

    get = lambda name: np.asarray(inputs[name])
    x = np.zeros((NP, DIM), np.float32)
    x[:NODES] = get("x")
    src = np.zeros(TILES * P, np.int32)
    src[:EDGES] = get("src")
    dst = np.full(TILES * P, NP - 1, np.int32)
    dst[:EDGES] = get("dst")
    attr = np.zeros((TILES * P, EDGE_DIM), np.float32)
    attr[:EDGES] = get("edge_attr_64")
    attr = attr.reshape(PAIRS, PW, EDGE_DIM).transpose(0, 2, 1)
    columns = ["L0_gnn_b1", "L0_gnn_g1", "L0_gnn_be1", "L0_gnn_b2", "L0_gnn_g2", "L0_gnn_be2", "L1_gnn_b3"]
    rows = ["L1_gnn_b1", "L1_gnn_b2", "L1_gnn_b4", "L1_gnn_gamma", "L1_gnn_beta"]
    arrays = {
        "x": x,
        "src_cols": src.reshape(TILES, P).T,
        "dst_cols": dst.reshape(TILES, P).T,
        "dst_rows": dst.reshape(TILES, P),
        "edge_attr_t": np.concatenate([attr, attr], axis=1),
        "eps": get("L0_gnn_eps").reshape(1),
        "cols": np.concatenate([get(n).reshape(-1, P).T for n in columns], axis=1),
        "rows": np.stack([get(n) for n in rows]),
        "w01": get("L0_gnn_W1"), "w02": get("L0_gnn_W2"),
        "w1": get("L1_gnn_W1"), "w2": get("L1_gnn_W2"), "w3": get("L1_gnn_W3"), "w4": get("L1_gnn_W4"),
    }
    nc = bacc.Bacc("TRN2", target_bir_lowering=False, num_devices=1)
    feeds, args = {}, {}
    for name, a in arrays.items():
        a = np.ascontiguousarray(a)
        feeds[f"in_{name}"] = a
        args[name] = nc.dram_tensor(f"in_{name}", a.shape, mybir.dt.from_np(a.dtype), kind="ExternalInput").ap()
    args["out"] = nc.dram_tensor("out_x", (NODES, DIM), F32, kind="ExternalOutput").ap()
    gnn_kernel(nc, **args)
    r = run_bass_kernel_spmd(nc, [feeds], core_ids=[0])
    return r.results[0]["out_x"]
```
